# Optimizing a Trainium2 kernel written in Bass

```python
import numpy as np
import jax
import jax.numpy as jnp

def _softmax(x, axis=-1):
    return jax.nn.softmax(x, axis=axis)
def _gelu(x):
    return jax.nn.gelu(x, approximate=True)
def _silu(x):
    return jax.nn.silu(x)
def _sigmoid(x):
    return jax.nn.sigmoid(x)
def _layernorm(x, axis=-1, eps=1e-5):
    m = jnp.mean(x, axis=axis, keepdims=True)
    v = jnp.var(x, axis=axis, keepdims=True)
    return (x - m) / jnp.sqrt(v + eps)
def _scatter_add(tgt, idx, src, axis=0):
    return tgt.at[idx].add(src)
def _segment_sum(src, seg, n):
    return jax.ops.segment_sum(src, seg, n)

kernel_name = 'mk_conv_preact_d1_conv_nhwc128_6d1b78'

def setup_inputs(seed: int = 0):
    np.random.seed(seed)
    _w = jnp.asarray
    def _rec_inputs():
        import jax
        import jax.numpy as jnp
        _gk = jax.random.key(seed)
        x = -0.000125 + 0.9999 * jax.random.normal(jax.random.fold_in(_gk, 1), (16, 64, 256, 128), jnp.float32)
        return x
    x = _rec_inputs()
    def _L0_conv_setup():
        import jax, jax.numpy as jnp
        import numpy as np
        NUM_HEAD = 2
        key = jax.random.key(seed)
        k1, k2, k3 = jax.random.split(key, 3)
        B, G, L, C = (16, 64, 256, 128)
        x = jax.random.normal(k1, (B, G, L, C), dtype=jnp.float32)
        W_qkv = jax.random.normal(k2, (3 * C, C), dtype=jnp.float32) * C ** (-0.5)
        b_qkv = jax.random.normal(k3, (3 * C,), dtype=jnp.float32) * 0.02
        return {'x': x, 'W_qkv': W_qkv, 'b_qkv': b_qkv}
    _L0_conv_all = _L0_conv_setup()
    _L0_conv_in = {k: v for k, v in _L0_conv_all.items() if k in ('W_qkv', 'b_qkv', )}
    del _L0_conv_all

    return {
        "x": x,
        "L0_conv_W_qkv": _L0_conv_in["W_qkv"],
        "L0_conv_b_qkv": _L0_conv_in["b_qkv"],
    }

def reference(x, L0_conv_W_qkv, L0_conv_b_qkv):
    import jax
    import jax.numpy as jnp
    def _L0_conv_ref(x, W_qkv, b_qkv):
        import jax, jax.numpy as jnp
        import numpy as np
        NUM_HEAD = 2
        B, G, L, C = x.shape
        H = NUM_HEAD
        c = C // H
        scale = C ** 0.5
        qkv = jnp.einsum('bglc,dc->bgld', x, W_qkv) + b_qkv
        qkv = qkv.reshape(B, G, L, 3, H, c).transpose(3, 0, 1, 4, 2, 5)
        q, k, v = (qkv[0], qkv[1], qkv[2])
        score = jnp.einsum('bghlc,bghmc->bghlm', q, k) / scale
        score = jax.nn.softmax(score, axis=-1)
        out = jnp.einsum('bghlm,bghmc->bghlc', score, v)
        out = out.transpose(0, 1, 3, 2, 4).reshape(B, G, L, C)
        return out

    def _gn(v, G=32, eps=1e-5):
        B_, H_, W_, C_ = v.shape
        g = v.reshape(B_, H_, W_, G, C_ // G)
        m = jnp.mean(g, axis=(1, 2, 4), keepdims=True)
        s = jnp.var(g, axis=(1, 2, 4), keepdims=True)
        return ((g - m) / jnp.sqrt(s + eps)).reshape(v.shape)

    def _ln_c(v, eps=1e-6):
        m = jnp.mean(v, axis=-1, keepdims=True)
        s = jnp.var(v, axis=-1, keepdims=True)
        return (v - m) / jnp.sqrt(s + eps)

    def _ln_t(v, eps=1e-5):
        m = jnp.mean(v, axis=-1, keepdims=True)
        s = jnp.var(v, axis=-1, keepdims=True)
        return (v - m) / jnp.sqrt(s + eps)

    def _to_tokens(v):
        B_, H_, W_, C_ = v.shape
        return v.reshape(B_, H_ * W_, C_)
    def _from_tokens(t, like):
        return t.reshape(like.shape)

    x = x + _L0_conv_ref(_gn(x), L0_conv_W_qkv, L0_conv_b_qkv)
    return x


_drawn_inputs = setup_inputs


def setup_inputs(seed=0):
    import zlib

    import numpy as np

    out = dict(_drawn_inputs(seed))
    spreads = {}
    factors = {}
    for name, (base, spread) in spreads.items():
        noise = np.random.default_rng([zlib.crc32(name.encode()), seed]).standard_normal(out[name].shape)
        drawn = base * np.exp(spread * noise) if base else spread * noise
        out[name] = jnp.asarray(drawn.astype(out[name].dtype))
    for name, factor in factors.items():
        out[name] = (out[name] * factor).astype(out[name].dtype)
    return out
```

```python
import math
from contextlib import ExitStack

import concourse.bass as bass
from concourse import mybir

F32 = mybir.dt.float32
F32R = mybir.dt.float32r
F16 = mybir.dt.float16
I32 = mybir.dt.int32
ALU = mybir.AluOpType
ACT = mybir.ActivationFunctionType
AX = mybir.AxisListType

P = 128
UNROLL = 4
P_SCALE = 2.0 ** 15
V_TOP = 2.0 ** 14
EPS = 1e-5


def groupnorm_attention(nc: bass.Bass, x: bass.AP, w: bass.AP, b: bass.AP, out: bass.AP):
    IMAGES, ROWS, TOK, C = x.shape
    HEADS, GROUPS = 2, 32
    HC = C // HEADS
    GC = C // GROUPS
    J = TOK // P
    BLOCKS = IMAGES * ROWS
    LAST = BLOCKS - 1
    SCALE = 1.0 / math.sqrt(C)
    NORM_COUNT = ROWS * TOK * GC
    HALF_COUNT = ROWS * J * GC // 2
    assert C == P and J == 2 and ROWS * J * GC == 512 and BLOCKS % UNROLL == 0
    PAIRS = ROWS // 2
    STATS_FROM = ROWS - UNROLL - GROUPS
    assert STATS_FROM % UNROLL == 0
    LOADS = 8
    LB = ROWS // LOADS

    x_img = x.rearrange("n r (p j) c -> n p r (j c)", j=J)
    out_pairs = out.rearrange("n (k r) (p j) c -> (n k) p r (j c)", r=2, j=J)

    with ExitStack() as ctx:
        def sb(name, shape, dt=F32):
            return ctx.enter_context(nc.sbuf_tensor(name, shape, dt))

        def bank(name):
            return ctx.enter_context(nc.psum_tensor(name, [P, 512], F32))

        def sem(name):
            return ctx.enter_context(nc.semaphore(name))

        image = sb("image", [P, 2, ROWS, J * C])
        x_ring = sb("x_ring", [P, 4, J * C])
        xb_ring = sb("xb_ring", [P, 4, J * C])
        y_ring = sb("y_ring", [P, 4, J * C])
        xn = sb("xn", [P, 2, TOK])
        xn_hi = sb("xn_hi", [P, 2, TOK], F32R)
        xn_lo = sb("xn_lo", [P, 2, TOK], F32R)
        qk_hi = sb("qk_hi", [P, 2, 2, TOK], F32R)
        qk_lo = sb("qk_lo", [P, 2, 2, TOK], F32R)
        prob = sb("prob", [P, 2, HEADS, J, TOK])
        p_hi = sb("p_hi", [P, 2, HEADS, J * TOK], F16)
        p_lo = sb("p_lo", [P, 2, HEADS, J * TOK], F16)
        v_hi = sb("v_hi", [P, 2, J, HEADS, HC + 1], F16)
        v_lo = sb("v_lo", [P, 2, J, HEADS, HC + 1], F16)
        neg_max = sb("neg_max", [P, 2, HEADS, J])
        rsum = sb("rsum", [P, 2, J * HEADS])
        o_norm = sb("o_norm", [P, 2, J, HEADS, HC])

        ident = sb("ident", [P, P])
        w_in = sb("w_in", [P, 3, C])
        b_in = sb("b_in", [P, 3])
        w_hi = sb("w_hi", [P, 3, C], F32R)
        w_lo = sb("w_lo", [P, 3, C], F32R)
        v_bound = sb("v_bound", [P, 4])
        spread = sb("spread", [P, 2, P])
        v_back = sb("v_back", [P, C])
        v_bias = sb("v_bias", [P, J, C])

        bn = sb("bn", [P, GROUPS, 2, 3])
        st = sb("st", [P, 6, GROUPS])
        dev = sb("dev", [P, GROUPS, 2])
        wide = sb("wide", [P, 2, GROUPS, GC])
        norm = sb("norm", [P, 2, 2])
        mean_of = sb("mean_of", [P, P])
        var_of = sb("var_of", [P, P])

        xt_bank = bank("xt_bank")
        qk_bank = bank("qk_bank")
        v_bank = bank("v_bank")
        s_bank = [bank(f"s_bank{h}") for h in range(HEADS)]
        t_bank = [bank(f"t_bank{h}") for h in range(HEADS)]
        o_bank = bank("o_bank")
        o_view = o_bank[:, 0:J * HEADS * (HC + 1)].rearrange("p (a c) -> p a c", c=HC + 1)

        loaded = [sem(f"loaded{i}") for i in range(2)]
        ring_in = [sem(f"ring_in{i}") for i in range(2)]
        stored = [sem(f"stored{i}") for i in range(2)]
        xt_done = sem("xt_done")
        xn_done = sem("xn_done")
        xhi_done = sem("xhi_done")
        xlo_done = sem("xlo_done")
        xb_done = sem("xb_done")
        qk_done = sem("qk_done")
        qkhi_done = sem("qkhi_done")
        qklo_done = sem("qklo_done")
        v_done = sem("v_done")
        vhi_done = sem("vhi_done")
        vlo_done = sem("vlo_done")
        s_done = sem("s_done")
        max_done = [sem(f"max_done{h}") for h in range(HEADS)]
        exp_done = [sem(f"exp_done{h}") for h in range(HEADS)]
        t_done = [sem(f"t_done{h}") for h in range(HEADS)]
        phi_done = [sem(f"phi_done{h}") for h in range(HEADS)]
        plo_done = [sem(f"plo_done{h}") for h in range(HEADS)]
        pv_done = sem("pv_done")
        rsum_done = sem("rsum_done")
        o_done = sem("o_done")
        y_done = sem("y_done")
        bn_done = sem("bn_done")
        stat_step = sem("stat_step")
        stat_mm = sem("stat_mm")
        w_loaded = sem("w_loaded")
        const_done = sem("const_done")
        setup_dve = sem("setup_dve")
        setup_pe = sem("setup_pe")

        STAT_STEPS = 21

        block = ctx.enter_context(nc.Block())

        def known_below(base, n):
            return isinstance(base, int) and base < n

        @block.sync
        def _(sp):
            def load_image(img, part, parity):
                rows = slice(part * LB, (part + 1) * LB)
                sp.dma_start(image[:, parity, rows, :], x_img[img, :, rows, :]).then_inc(loaded[parity], 16)

            def refill(g0, row0, parity, k):
                if not known_below(g0, UNROLL):
                    sp.wait_ge(xt_done, g0 + (2 * k + 2 - 4))
                    sp.wait_ge(xb_done, g0 + (2 * k + 2 - 4))
                sp.dma_start(x_ring[:, 2 * k:2 * k + 2, :],
                             image[:, parity, bass.ds(row0 + 2 * k, 2), :]).then_inc(ring_in[k], 16)

            def store(g0, pair0, k):
                sp.wait_ge(y_done, g0 + (2 * k + 2))
                sp.dma_start(out_pairs[bass.ds(pair0 + k, 1)].rearrange("a p r c -> (a p) r c"),
                             y_ring[:, 2 * k:2 * k + 2, :]).then_inc(stored[k], 16)

            sp.dma_start(w_in[:, :, :], w.rearrange("(t d) c -> d t c", d=P)).then_inc(w_loaded, 16)
            for t in range(3):
                sp.dma_start(b_in[:, t:t + 1], b[t * P:(t + 1) * P].rearrange("(d a) -> d a", a=1)).then_inc(w_loaded, 16)
            for part in range(LOADS):
                load_image(0, part, 0)

            def run_image(img, par, is_first, is_last):
                g = img * ROWS
                if is_first:
                    sp.wait_ge(loaded[par], 16 * LOADS)
                    refill(0, 0, par, 0)
                    refill(0, 0, par, 1)
                if not is_last:
                    if not is_first:
                        for k in range(2):
                            sp.wait_ge(ring_in[k], 4 * g)
                    for part in range(LOADS):
                        load_image(img + 1, part, 1 - par)
                with sp.Fori(0, ROWS // UNROLL - 1) as t:
                    for k in range(2):
                        refill(t * UNROLL + g + UNROLL, t * UNROLL + UNROLL, par, k)
                    for k in range(2):
                        store(t * UNROLL + g, t * 2 + img * PAIRS, k)
                if not is_last:
                    for k in range(2):
                        refill(g + ROWS, 0, 1 - par, k)
                for k in range(2):
                    store(g + (ROWS - UNROLL), img * PAIRS + (PAIRS - 2), k)

            run_image(0, 0, True, False)
            with sp.Fori(0, IMAGES // 2 - 1) as q:
                for s in range(2):
                    run_image(q * 2 + (1 + s), 1 - s, False, False)
            run_image(IMAGES - 1, (IMAGES - 1) % 2, False, True)
            for k in range(2):
                sp.wait_ge(stored[k], 16 * BLOCKS // 4)

        def schedule(eng, step):
            def run_image(img, par, first, last):
                g = img * ROWS
                start = 0
                if first:
                    for u in range(UNROLL):
                        step(g, u, par, u, None)
                    start = UNROLL
                with eng.Fori(0, (STATS_FROM - start) // UNROLL) as t:
                    for u in range(UNROLL):
                        step(t * UNROLL + g + start, u, par, None, None)
                with eng.Fori(0, GROUPS // UNROLL) as t:
                    for u in range(UNROLL):
                        step(t * UNROLL + g + STATS_FROM, u, par, None,
                             None if last else ("measure", g, t * UNROLL + u))
                for u in range(UNROLL):
                    step(g + (ROWS - UNROLL), u, par, ROWS - UNROLL + u, None if last else ("finish", img + 1))

            run_image(0, 0, True, False)
            with eng.Fori(0, IMAGES // 2 - 1) as q:
                for s in range(2):
                    run_image(q * 2 + (1 + s), 1 - s, False, False)
            run_image(IMAGES - 1, (IMAGES - 1) % 2, False, True)

        def ahead(base, u, row, par, n):
            if isinstance(base, int) and base + u + n > LAST:
                return None
            return 1 - par if row is not None and row + n >= ROWS else par

        def split(base, v):
            return base + v // UNROLL * UNROLL, v % UNROLL

        @block.tensor
        def _(pe):
            def x_transpose(base, v):
                g, m = split(base, v)
                pe.wait_ge(ring_in[m // 2], 4 * g + 16)
                if not known_below(base, 1 - v):
                    pe.wait_ge(xn_done, base + v)
                for j in range(J):
                    mm = pe.transpose(xt_bank[:, j * P:(j + 1) * P], x_ring[:, m, j * C:(j + 1) * C], ident[:, :])
                mm.then_inc(xt_done, 1)

            def project_qk(base, v):
                pe.wait_ge(xlo_done, base + (v + 1))
                if not known_below(base, 1 - v):
                    pe.wait_ge(qklo_done, base + v)
                m = v % 2
                for t in range(2):
                    o = qk_bank[:, t * TOK:(t + 1) * TOK]
                    pe.matmul(o, w_lo[:, t, :], xn_hi[:, m, :], start=True, stop=False)
                    pe.matmul(o, w_hi[:, t, :], xn_lo[:, m, :], start=False, stop=False)
                    mm = pe.matmul(o, w_hi[:, t, :], xn_hi[:, m, :], start=False, stop=True)
                mm.then_inc(qk_done, 1)

            def project_v(base, v):
                if not known_below(base, 1 - v):
                    pe.wait_ge(vlo_done, base + v)
                m = v % 2
                for j in range(J):
                    o = v_bank[:, j * C:(j + 1) * C]
                    c = slice(j * P, (j + 1) * P)
                    pe.matmul(o, xn_lo[:, m, c], w_hi[:, 2, :], start=True, stop=False)
                    pe.matmul(o, xn_hi[:, m, c], w_lo[:, 2, :], start=False, stop=False)
                    mm = pe.matmul(o, xn_hi[:, m, c], w_hi[:, 2, :], start=False, stop=True)
                mm.then_inc(v_done, 1)

            def scores(base, v):
                pe.wait_ge(qklo_done, base + (v + 1))
                if not known_below(base, 1 - v):
                    for h in range(HEADS):
                        pe.wait_ge(exp_done[h], base + v)
                m = v % 2
                for a in range(J):
                    for n, (q, k) in enumerate(((qk_lo, qk_hi), (qk_hi, qk_lo), (qk_hi, qk_hi))):
                        for h in range(HEADS):
                            c = slice(h * HC, (h + 1) * HC)
                            mm = pe.matmul(s_bank[h][:, a * TOK:(a + 1) * TOK], q[c, m, 0, a * P:(a + 1) * P],
                                           k[c, m, 1, :], start=(n == 0), stop=(n == 2))
                mm.then_inc(s_done, 1)

            def p_transpose(base, v, h):
                pe.wait_ge(exp_done[h], base + (v + 1))
                if not known_below(base, 1 - v):
                    pe.wait_ge(plo_done[h], base + v)
                for j in range(J):
                    for a in range(J):
                        mm = pe.transpose(t_bank[h][:, j * TOK + a * P:j * TOK + (a + 1) * P],
                                          prob[:, v % 2, h, a, j * P:(j + 1) * P], ident[:, :])
                mm.then_inc(t_done[h], 1)

            def values(base, v):
                pe.wait_ge(vlo_done, base + (v + 1))
                if not known_below(base, 1 - v):
                    pe.wait_ge(o_done, base + v)
                m = v % 2
                for h in range(HEADS):
                    pe.wait_ge(plo_done[h], base + (v + 1))
                    for a in range(J):
                        for j in range(J):
                            c = slice(j * TOK + a * P, j * TOK + (a + 1) * P)
                            for n, (pp, vv) in enumerate(((p_lo, v_hi), (p_hi, v_lo), (p_hi, v_hi))):
                                mm = pe.matmul(o_view[:, a * HEADS + h, :], pp[:, m, h, c], vv[:, m, j, h, :],
                                               start=(j == 0 and n == 0), stop=(j == J - 1 and n == 2))
                mm.then_inc(pv_done, 1)

            def statistics(n, part):
                if part == 0:
                    pe.wait_ge(stat_step, n + 1)
                    pe.matmul(xt_bank[:, 256:256 + GROUPS], mean_of[:, :], st[:, 0, :],
                              start=True, stop=True).then_inc(stat_mm, 1)
                elif part == 1:
                    pe.wait_ge(stat_step, n + 6)
                    pe.matmul(xt_bank[:, 256:256 + GROUPS], var_of[:, :], st[:, 3, :],
                              start=True, stop=True).then_inc(stat_mm, 1)
                else:
                    pe.wait_ge(stat_step, n + 20)
                    for i in range(2):
                        mm = pe.transpose(xt_bank[:, 256 + i * P:256 + (i + 1) * P],
                                          wide[:, i, :, :].rearrange("p g c -> p (g c)"), ident[:, :])
                    mm.then_inc(stat_mm, 1)

            pe.wait_ge(const_done, 8)
            pe.wait_ge(setup_dve, 9)
            for t in range(3):
                pe.transpose(s_bank[0][:, t * P:(t + 1) * P], w_in[:, t, :], ident[:, :])
            for i in range(2):
                mm = pe.transpose(s_bank[1][:, i * P:(i + 1) * P], spread[:, i, :], ident[:, :])
            mm.then_inc(setup_pe, 1)
            for part in range(3):
                statistics(0, part)
            pe.wait_ge(stat_step, STAT_STEPS)
            pe.wait_ge(setup_dve, 13)
            x_transpose(0, 0)
            x_transpose(0, 1)
            project_qk(0, 0)
            project_v(0, 0)

            def step(base, u, par, row, stats):
                scores(base, u)
                if ahead(base, u, row, par, 1) is not None:
                    project_qk(base, u + 1)
                if not known_below(base, 1 - u):
                    values(base, u - 1)
                if ahead(base, u, row, par, 1) is not None:
                    project_v(base, u + 1)
                p_transpose(base, u, 0)
                if stats is not None and stats[0] == "finish" and u < 3:
                    pe.wait_ge(xn_done, base + (u + 2))
                    statistics(stats[1] * STAT_STEPS, u)
                    pe.wait_ge(stat_step, stats[1] * STAT_STEPS + (2, 8, STAT_STEPS)[u])
                if ahead(base, u, row, par, 2) is not None:
                    x_transpose(base, u + 2)
                p_transpose(base, u, 1)

            schedule(pe, step)
            values(LAST - UNROLL + 1, UNROLL - 1)

        @block.scalar
        def _(act):
            def x_high(base, v):
                m = v % 2
                act.wait_ge(xn_done, base + (v + 1))
                if not known_below(base, 2 - v):
                    act.wait_ge(v_done, base + (v - 1))
                act.activation(xn_hi[:, m, :], xn[:, m, :], ACT.Copy).then_inc(xhi_done, 1)

            def qk_high(base, v):
                m = v % 2
                act.wait_ge(qk_done, base + (v + 1))
                if not known_below(base, 2 - v):
                    act.wait_ge(s_done, base + (v - 1))
                for t in range(2):
                    ins = act.activation(qk_hi[:, m, t, :], qk_bank[:, t * TOK:(t + 1) * TOK], ACT.Identity,
                                         bias=b_in[:, t:t + 1])
                ins.then_inc(qkhi_done, 1)

            def v_high(base, v):
                act.wait_ge(v_done, base + (v + 1))
                if not known_below(base, 2 - v):
                    act.wait_ge(pv_done, base + (v - 1))
                act.activation(v_hi[:, v % 2, :, :, 0:HC],
                               v_bank[:, 0:J * C].rearrange("p (j h c) -> p j h c", j=J, h=HEADS),
                               ACT.Copy).then_inc(vhi_done, 1)

            def exponent(base, v, h):
                m = v % 2
                act.wait_ge(max_done[h], base + (v + 1))
                if not known_below(base, 2 - v):
                    act.wait_ge(t_done[h], base + (v - 1))
                for a in range(J):
                    ins = act.activation(prob[:, m, h, a, :], s_bank[h][:, a * TOK:(a + 1) * TOK], ACT.Exp,
                                         bias=neg_max[:, m, h, a:a + 1])
                ins.then_inc(exp_done[h], 1)

            def p_high(base, v, h):
                act.wait_ge(t_done[h], base + (v + 1))
                if not known_below(base, 2 - v):
                    act.wait_ge(pv_done, base + (v - 1))
                act.activation(p_hi[:, v % 2, h, :], t_bank[h][:, :], ACT.Copy,
                               scale=P_SCALE).then_inc(phi_done[h], 1)

            act.wait_ge(setup_dve, 13)
            x_high(0, 0)
            x_high(0, 1)
            qk_high(0, 0)
            v_high(0, 0)

            def step(base, u, par, row, stats):
                exponent(base, u, 0)
                if ahead(base, u, row, par, 1) is not None:
                    qk_high(base, u + 1)
                exponent(base, u, 1)
                if ahead(base, u, row, par, 1) is not None:
                    v_high(base, u + 1)
                p_high(base, u, 0)
                if ahead(base, u, row, par, 2) is not None:
                    x_high(base, u + 2)
                p_high(base, u, 1)

            schedule(act, step)

        @block.vector
        def _(dve):
            def normalise(base, v, par):
                m = v % 2
                dve.wait_ge(xt_done, base + (v + 1))
                if not known_below(base, 2 - v):
                    dve.wait_ge(xlo_done, base + (v - 1))
                dve.tensor_scalar(xn[:, m, :], xt_bank[:, 0:TOK], norm[:, par, 0:1], norm[:, par, 1:2],
                                  ALU.subtract, ALU.mult).then_inc(xn_done, 1)

            def qk_low(base, v):
                m = v % 2
                dve.wait_ge(qkhi_done, base + (v + 1))
                for t in range(2):
                    ins = dve.scalar_tensor_tensor(out=qk_lo[:, m, t, :], in0=qk_bank[:, t * TOK:(t + 1) * TOK],
                                                   scalar=b_in[:, t:t + 1], in1=qk_hi[:, m, t, :].bitcast(F32),
                                                   op0=ALU.add, op1=ALU.subtract)
                ins.then_inc(qklo_done, 1)

            def v_low(base, v):
                m = v % 2
                dve.wait_ge(vhi_done, base + (v + 1))
                dve.tensor_tensor(v_lo[:, m, :, :, 0:HC],
                                  v_bank[:, 0:J * C].rearrange("p (j h c) -> p j h c", j=J, h=HEADS),
                                  v_hi[:, m, :, :, 0:HC], ALU.subtract).then_inc(vlo_done, 1)

            def row_max(base, v, h):
                m = v % 2
                if h == 0:
                    dve.wait_ge(s_done, base + (v + 1))
                dve.tensor_reduce(neg_max[:, m, h, :], s_bank[h][:, :].rearrange("p (a k) -> p a k", a=J),
                                  AX.X, ALU.max, negate=True).then_inc(max_done[h], 1)

            def p_low(base, v, h):
                dve.wait_ge(phi_done[h], base + (v + 1))
                dve.scalar_tensor_tensor(out=p_lo[:, v % 2, h, :], in0=t_bank[h][:, :], scalar=P_SCALE,
                                         in1=p_hi[:, v % 2, h, :], op0=ALU.mult,
                                         op1=ALU.subtract).then_inc(plo_done[h], 1)

            def sums(base, v):
                dve.wait_ge(pv_done, base + (v + 1))
                dve.reciprocal(rsum[:, v % 2, :], o_view[:, :, HC]).then_inc(rsum_done, 1)

            def divide(base, v):
                m = v % 2
                dve.wait_ge(rsum_done, base + (v + 1))
                if not known_below(base, 2 - v):
                    dve.wait_ge(y_done, base + (v - 1))
                for a in range(J):
                    for h in range(HEADS):
                        n = a * HEADS + h
                        ins = dve.scalar_tensor_tensor(out=o_norm[:, m, a, h, :], in0=o_view[:, n, 0:HC],
                                                       scalar=rsum[:, m, n:n + 1], in1=v_back[:, h * HC:(h + 1) * HC],
                                                       op0=ALU.mult, op1=ALU.mult)
                ins.then_inc(o_done, 1)

            def measure(group, par):
                dve.bn_stats(bn[:, bass.ds(group, 1), :, :].rearrange("p g a b -> p (g a b)"),
                             image[:, par, :, :].rearrange("p r (j c) -> p (r j) c", j=J)[:, :, bass.ds(group * GC, GC)]
                             ).then_inc(bn_done, 1)

            def statistics(n, images, par, part):
                at = [n + (0, 2, 8)[part]]

                def chain(ins):
                    at[0] = at[0] + 1
                    ins.then_inc(stat_step, 1)
                    dve.wait_ge(stat_step, at[0])

                if part == 0:
                    dve.wait_ge(bn_done, (images + 1) * GROUPS)
                    chain(dve.tensor_tensor(st[:, 0, :], bn[:, :, 0, 1], bn[:, :, 1, 1], ALU.add))
                    dve.wait_ge(stat_mm, images * 3 + 1)
                    chain(dve.tensor_copy(st[:, 1, :], xt_bank[:, 256:256 + GROUPS]))
                elif part == 1:
                    chain(dve.tensor_tensor(dev[:, :, :], bn[:, :, :, 1],
                                            st[:, 1, :].unsqueeze(2).broadcast_to([P, GROUPS, 2]), ALU.subtract))
                    chain(dve.tensor_tensor(dev[:, :, :], dev[:, :, :], dev[:, :, :], ALU.mult))
                    chain(dve.scalar_tensor_tensor(out=dev[:, :, :], in0=dev[:, :, :], scalar=float(HALF_COUNT),
                                                   in1=bn[:, :, :, 2], op0=ALU.mult, op1=ALU.add))
                    chain(dve.tensor_tensor(st[:, 3, :], dev[:, :, 0], dev[:, :, 1], ALU.add))
                    chain(dve.tensor_copy(wide[:, 0, :, :],
                                          st[:, 1, :].unsqueeze(2).broadcast_to([P, GROUPS, GC])))
                    dve.wait_ge(stat_mm, images * 3 + 2)
                    chain(dve.tensor_scalar(st[:, 4, :], xt_bank[:, 256:256 + GROUPS], EPS, None, ALU.add))
                else:
                    chain(dve.tensor_scalar(st[:, 2, :].bitcast(I32), st[:, 4, :].bitcast(I32), 1, None,
                                            ALU.logical_shift_right))
                    chain(dve.tensor_scalar(st[:, 5, :].bitcast(I32), st[:, 2, :].bitcast(I32), -1.0,
                                            float(0x5F3759DF), ALU.mult, ALU.add))
                    for _ in range(3):
                        chain(dve.tensor_tensor(st[:, 2, :], st[:, 5, :], st[:, 5, :], ALU.mult))
                        chain(dve.scalar_tensor_tensor(out=st[:, 2, :], in0=st[:, 2, :], scalar=-0.5,
                                                       in1=st[:, 4, :], op0=ALU.mult, op1=ALU.mult))
                        chain(dve.scalar_tensor_tensor(out=st[:, 5, :], in0=st[:, 2, :], scalar=1.5,
                                                       in1=st[:, 5, :], op0=ALU.add, op1=ALU.mult))
                    chain(dve.tensor_copy(wide[:, 1, :, :],
                                          st[:, 5, :].unsqueeze(2).broadcast_to([P, GROUPS, GC])))
                    dve.wait_ge(stat_mm, images * 3 + 3)
                    chain(dve.tensor_copy(norm[:, par, :],
                                          xt_bank[:, 256:512].rearrange("p (i q) -> p i q", i=2)[:, :, 0]))

            n = [0]

            def chain(ins):
                n[0] += 1
                ins.then_inc(setup_dve, 1)
                dve.wait_ge(setup_dve, n[0])

            dve.wait_ge(w_loaded, 64)
            dve.tensor_reduce(v_bound[:, 0:1], w_in[:, 2, :], AX.X, ALU.add, apply_absolute_value=True)\
                .then_inc(setup_dve, 1)
            n[0] += 1
            chain(dve.tensor_scalar(w_in[:, 0, :], w_in[:, 0, :], SCALE, None, ALU.mult))
            chain(dve.tensor_scalar(v_bound[:, 1:2], v_bound[:, 0:1], math.sqrt(NORM_COUNT), 2.0 ** -60,
                                    ALU.mult, ALU.max))
            chain(dve.tensor_scalar(v_bound[:, 2:3].bitcast(I32), v_bound[:, 1:2].bitcast(I32), 0x7F800000, None,
                                    ALU.bitwise_and))
            chain(dve.tensor_scalar(v_bound[:, 2:3], v_bound[:, 2:3], 1.0 / V_TOP, None, ALU.mult))
            chain(dve.reciprocal(v_bound[:, 3:4], v_bound[:, 2:3]))
            chain(dve.tensor_scalar(w_in[:, 2, :], w_in[:, 2, :], v_bound[:, 3:4], None, ALU.mult))
            dve.wait_ge(const_done, 4)
            chain(dve.tensor_scalar(spread[:, 0, :], mean_of[:, :], 0.0, v_bound[:, 2:3], ALU.mult, ALU.add))
            chain(dve.tensor_scalar(spread[:, 1, :], mean_of[:, :], 0.0, b_in[:, 2:3], ALU.mult, ALU.add))
            dve.wait_ge(setup_pe, 1)
            chain(dve.tensor_copy(w_hi[:, :, :], s_bank[0][:, 0:3 * P].rearrange("p (t c) -> p t c", t=3)))
            chain(dve.tensor_tensor(w_lo[:, :, :], s_bank[0][:, 0:3 * P].rearrange("p (t c) -> p t c", t=3),
                                    w_hi[:, :, :].bitcast(F32), ALU.subtract))
            chain(dve.tensor_copy(v_back[:, :], s_bank[1][:, 0:P]))
            dve.tensor_scalar(b_in[:, 0:1], b_in[:, 0:1], SCALE, None, ALU.mult).then_inc(setup_dve, 1)
            n[0] += 1
            for j in range(J):
                chain(dve.tensor_copy(v_bias[:, j, :], s_bank[1][:, P:2 * P]))
            assert n[0] == 15

            dve.wait_ge(loaded[0], 16 * LOADS)
            for group in range(GROUPS):
                measure(group, 0)
            for part in range(3):
                statistics(0, 0, 0, part)
            normalise(0, 0, 0)
            normalise(0, 1, 0)
            qk_low(0, 0)
            v_low(0, 0)

            def step(base, u, par, row, stats):
                row_max(base, u, 0)
                row_max(base, u, 1)
                if not known_below(base, 1 - u):
                    sums(base, u - 1)
                if stats is not None and stats[0] == "measure":
                    g = stats[1]
                    if u == 0:
                        dve.wait_ge(loaded[1 - par], (g + ROWS * par) * (16 * LOADS // (2 * ROWS)) + 16 * LOADS)
                    measure(stats[2], 1 - par)
                if not known_below(base, 1 - u):
                    divide(base, u - 1)
                if ahead(base, u, row, par, 1) is not None:
                    qk_low(base, u + 1)
                    v_low(base, u + 1)
                p_low(base, u, 0)
                if stats is not None and stats[0] == "finish" and u < 3:
                    statistics(stats[1] * STAT_STEPS, stats[1], 1 - par, u)
                nxt = ahead(base, u, row, par, 2)
                if nxt is not None:
                    normalise(base, u + 2, nxt)
                p_low(base, u, 1)

            schedule(dve, step)
            sums(LAST - UNROLL + 1, UNROLL - 1)
            divide(LAST - UNROLL + 1, UNROLL - 1)

        @block.gpsimd
        def _(pool):
            def x_low(base, v):
                m = v % 2
                pool.wait_ge(xhi_done, base + (v + 1))
                pool.tensor_tensor(xn_lo[:, m, :], xn[:, m, :], xn_hi[:, m, :].bitcast(F32),
                                   ALU.subtract).then_inc(xlo_done, 1)

            def add_bias(base, v):
                g, m = split(base, v)
                pool.wait_ge(ring_in[m // 2], 4 * g + 16)
                if not known_below(base, 4 - v):
                    pool.wait_ge(y_done, base + (v - 3))
                pool.tensor_tensor(xb_ring[:, m, :], x_ring[:, m, :],
                                   v_bias[:, :, :].rearrange("p j c -> p (j c)"), ALU.add).then_inc(xb_done, 1)

            def finish(base, v):
                g, m = split(base, v)
                pool.wait_ge(o_done, base + (v + 1))
                pool.wait_ge(xb_done, base + (v + 1))
                if not known_below(base, 4 - v):
                    pool.wait_ge(stored[m // 2], 4 * g)
                pool.tensor_tensor(y_ring[:, m, :], xb_ring[:, m, :],
                                   o_norm[:, v % 2, :, :, :].rearrange("p j h c -> p (j h c)"),
                                   ALU.add).then_inc(y_done, 1)

            pool.memset(ident[:, :], 0.0).then_inc(const_done, 1)
            pool.memset(mean_of[:, :], 1.0 / (2 * P)).then_inc(const_done, 1)
            pool.memset(var_of[:, :], 1.0 / NORM_COUNT).then_inc(const_done, 1)
            pool.wait_ge(const_done, 3)
            pool.affine_select(out=ident[:, :], in_=ident[:, :], compare_op=ALU.not_equal, fill=1.0, base=0,
                               pattern=[[-1, P]], channel_multiplier=1).then_inc(const_done, 1)
            for m in range(2):
                pool.memset(v_hi[:, m, :, :, HC:HC + 1], 1.0).then_inc(const_done, 1)
                pool.memset(v_lo[:, m, :, :, HC:HC + 1], 0.0).then_inc(const_done, 1)
            pool.wait_ge(setup_dve, 15)
            add_bias(0, 0)
            add_bias(0, 1)
            x_low(0, 0)
            x_low(0, 1)

            def step(base, u, par, row, stats):
                if not known_below(base, 1 - u):
                    finish(base, u - 1)
                if ahead(base, u, row, par, 2) is not None:
                    add_bias(base, u + 2)
                    x_low(base, u + 2)

            schedule(pool, step)
            finish(LAST - UNROLL + 1, UNROLL - 1)


_INS = ["x", "L0_conv_W_qkv", "L0_conv_b_qkv"]


def kernel(**inputs):
    import numpy as _np
    import concourse.bacc as _bacc
    from concourse import mybir as _mybir
    from concourse.bass_utils import run_bass_kernel_spmd as _run

    nc = _bacc.Bacc("TRN2", target_bir_lowering=False, num_devices=1)
    arrays, args = {}, []
    for name in _INS:
        a = _np.ascontiguousarray(inputs[name])
        arrays[f"in_{name}_dram"] = a
        args.append(nc.dram_tensor(f"in_{name}_dram", a.shape, _mybir.dt.from_np(a.dtype), kind="ExternalInput").ap())
    shape = inputs["x"].shape
    args.append(nc.dram_tensor("out_0_dram", shape, _mybir.dt.float32, kind="ExternalOutput").ap())
    groupnorm_attention(nc, *args)
    r = _run(nc, [arrays], core_ids=[0])
    return r.results[0]["out_0_dram"]
```

```python
import math
from contextlib import ExitStack

import concourse.bass as bass
from concourse import mybir

F32 = mybir.dt.float32
F32R = mybir.dt.float32r
F16 = mybir.dt.float16
I32 = mybir.dt.int32
ALU = mybir.AluOpType
ACT = mybir.ActivationFunctionType
AX = mybir.AxisListType

P = 128
UNROLL = 4
P_SCALE = 2.0 ** 15
V_TOP = 2.0 ** 14
EPS = 1e-5


def groupnorm_attention(nc: bass.Bass, x: bass.AP, w: bass.AP, b: bass.AP, out: bass.AP):
    IMAGES, ROWS, TOK, C = x.shape
    HEADS, GROUPS = 2, 32
    HC = C // HEADS
    GC = C // GROUPS
    J = TOK // P
    BLOCKS = IMAGES * ROWS
    LAST = BLOCKS - 1
    SCALE = 1.0 / math.sqrt(C)
    NORM_COUNT = ROWS * TOK * GC
    HALF_COUNT = ROWS * J * GC // 2
    assert C == P and J == 2 and ROWS * J * GC == 512 and BLOCKS % UNROLL == 0
    PAIRS = ROWS // 2
    STATS_FROM = ROWS - UNROLL - GROUPS
    assert STATS_FROM % UNROLL == 0
    LOADS = 8
    LB = ROWS // LOADS

    x_img = x.rearrange("n r (p j) c -> n p r (j c)", j=J)
    out_pairs = out.rearrange("n (k r) (p j) c -> (n k) p r (j c)", r=2, j=J)

    with ExitStack() as ctx:
        def sb(name, shape, dt=F32):
            return ctx.enter_context(nc.sbuf_tensor(name, shape, dt))

        def bank(name):
            return ctx.enter_context(nc.psum_tensor(name, [P, 512], F32))

        def sem(name):
            return ctx.enter_context(nc.semaphore(name))

        image = sb("image", [P, 2, ROWS, J * C])
        x_ring = sb("x_ring", [P, 4, J * C])
        xb_ring = sb("xb_ring", [P, 4, J * C])
        y_ring = sb("y_ring", [P, 4, J * C])
        xc_hi = sb("xc_hi", [P, 2, TOK], F32R)
        xc_lo = sb("xc_lo", [P, 2, TOK], F32R)
        qk_hi = sb("qk_hi", [P, 2, 2, TOK], F32R)
        qk_lo = sb("qk_lo", [P, 2, 2, TOK], F32R)
        prob = sb("prob", [P, 2, HEADS, J, TOK])
        p_hi = sb("p_hi", [P, 2, HEADS, J * TOK], F16)
        p_lo = sb("p_lo", [P, 2, HEADS, J * TOK], F16)
        v_full = sb("v_full", [P, 2, J, HEADS, HC])
        v_hi = sb("v_hi", [P, 4, J, HEADS, HC + 1], F16)
        v_lo = sb("v_lo", [P, 4, J, HEADS, HC + 1], F16)
        neg_max = sb("neg_max", [P, 2, HEADS, J])
        rsum = sb("rsum", [P, 2, J * HEADS])
        o_norm = sb("o_norm", [P, 2, J * HEADS, HC])
        o_back = sb("o_back", [P, 2, J * HEADS * HC])

        ident = sb("ident", [P, P])
        w_in = sb("w_in", [P, 3, C])
        b_in = sb("b_in", [P, 3])
        w_t = sb("w_t", [P, 3, C])
        w_norm = sb("w_norm", [P, 3, C])
        w_hi = sb("w_hi", [P, 2, 3, C], F32R)
        w_lo = sb("w_lo", [P, 2, 3, C], F32R)
        v_bound = sb("v_bound", [P, 4])
        spread = sb("spread", [P, 2, P])
        v_back = sb("v_back", [P, J, C])
        v_bias = sb("v_bias", [P, J, C])

        bn = sb("bn", [P, GROUPS, 2, 3])
        st = sb("st", [P, 6, GROUPS])
        dev = sb("dev", [P, GROUPS, 2])
        wide = sb("wide", [P, 2, GROUPS, GC])
        norm = sb("norm", [P, 2, 2])
        mean_of = sb("mean_of", [P, P])
        var_of = sb("var_of", [P, P])

        xt_bank = bank("xt_bank")
        qk_bank = bank("qk_bank")
        v_bank = bank("v_bank")
        s_bank = [bank(f"s_bank{h}") for h in range(HEADS)]
        t_bank = [bank(f"t_bank{h}") for h in range(HEADS)]
        o_bank = bank("o_bank")
        o_view = o_bank[:, 0:J * HEADS * (HC + 1)].rearrange("p (a c) -> p a c", c=HC + 1)

        loaded = [sem(f"loaded{i}") for i in range(2)]
        ring_in = [sem(f"ring_in{i}") for i in range(2)]
        stored = [sem(f"stored{i}") for i in range(2)]
        xt_done = sem("xt_done")
        xhi_done = sem("xhi_done")
        xlo_done = sem("xlo_done")
        xb_done = sem("xb_done")
        qk_done = sem("qk_done")
        qkhi_done = sem("qkhi_done")
        qklo_done = sem("qklo_done")
        v_done = sem("v_done")
        vhi_done = sem("vhi_done")
        vlo_done = sem("vlo_done")
        s_done = sem("s_done")
        max_done = [sem(f"max_done{h}") for h in range(HEADS)]
        exp_done = [sem(f"exp_done{h}") for h in range(HEADS)]
        t_done = [sem(f"t_done{h}") for h in range(HEADS)]
        phi_done = [sem(f"phi_done{h}") for h in range(HEADS)]
        plo_done = [sem(f"plo_done{h}") for h in range(HEADS)]
        pv_done = sem("pv_done")
        rsum_done = sem("rsum_done")
        o_done = sem("o_done")
        back_done = sem("back_done")
        y_done = sem("y_done")
        bn_done = sem("bn_done")
        stat_step = sem("stat_step")
        stat_mm = sem("stat_mm")
        w_loaded = sem("w_loaded")
        const_done = sem("const_done")
        setup_dve = sem("setup_dve")
        setup_pe = sem("setup_pe")

        STAT_STEPS = 24

        block = ctx.enter_context(nc.Block())

        def known_below(base, n):
            return isinstance(base, int) and base < n

        @block.sync
        def _(sp):
            def load_image(img, part, parity):
                rows = slice(part * LB, (part + 1) * LB)
                sp.dma_start(image[:, parity, rows, :], x_img[img, :, rows, :]).then_inc(loaded[parity], 16)

            def refill(g0, row0, parity, k):
                if not known_below(g0, UNROLL):
                    sp.wait_ge(xt_done, g0 + (2 * k + 2 - 4))
                    sp.wait_ge(xb_done, g0 + (2 * k + 2 - 4))
                sp.dma_start(x_ring[:, 2 * k:2 * k + 2, :],
                             image[:, parity, bass.ds(row0 + 2 * k, 2), :]).then_inc(ring_in[k], 16)

            def store(g0, pair0, k):
                sp.wait_ge(y_done, g0 + (2 * k + 2))
                sp.dma_start(out_pairs[bass.ds(pair0 + k, 1)].rearrange("a p r c -> (a p) r c"),
                             y_ring[:, 2 * k:2 * k + 2, :]).then_inc(stored[k], 16)

            sp.dma_start(w_in[:, :, :], w.rearrange("(t d) c -> d t c", d=P)).then_inc(w_loaded, 16)
            for t in range(3):
                sp.dma_start(b_in[:, t:t + 1], b[t * P:(t + 1) * P].rearrange("(d a) -> d a", a=1)).then_inc(w_loaded, 16)
            for part in range(LOADS):
                load_image(0, part, 0)

            def run_image(img, par, is_first, is_last):
                g = img * ROWS
                if is_first:
                    sp.wait_ge(loaded[par], 16 * LOADS)
                    refill(0, 0, par, 0)
                    refill(0, 0, par, 1)
                if not is_last:
                    if not is_first:
                        for k in range(2):
                            sp.wait_ge(ring_in[k], 4 * g)
                    for part in range(LOADS):
                        load_image(img + 1, part, 1 - par)
                start = 0
                if is_first:
                    for k in range(2):
                        refill(UNROLL, UNROLL, par, k)
                    start = 1
                with sp.Fori(0, ROWS // UNROLL - 1 - start) as t:
                    for k in range(2):
                        refill(t * UNROLL + g + (1 + start) * UNROLL, t * UNROLL + (1 + start) * UNROLL, par, k)
                        store(t * UNROLL + g + (start - 1) * UNROLL, t * 2 + img * PAIRS + 2 * (start - 1), k)
                for k in range(2):
                    if not is_last:
                        refill(g + ROWS, 0, 1 - par, k)
                    store(g + (ROWS - 2 * UNROLL), img * PAIRS + (PAIRS - 4), k)
                if is_last:
                    for k in range(2):
                        store(g + (ROWS - UNROLL), img * PAIRS + (PAIRS - 2), k)

            run_image(0, 0, True, False)
            with sp.Fori(0, IMAGES // 2 - 1) as q:
                for s in range(2):
                    run_image(q * 2 + (1 + s), 1 - s, False, False)
            run_image(IMAGES - 1, (IMAGES - 1) % 2, False, True)
            for k in range(2):
                sp.wait_ge(stored[k], 16 * BLOCKS // 4)

        def schedule(eng, order, share=None):
            def step(base, u, par, row=None, what=None):
                def run(lead, stage, *head):
                    v = u + lead
                    if isinstance(base, int) and not 0 <= base + v <= LAST:
                        return
                    stage(*head, base, v, par if row is None or 0 <= row + lead < ROWS else 1 - par)

                def measuring():
                    if what is not None:
                        share(base, u, par, what)

                order(run, measuring)

            def run_image(img, par, first, last):
                g = img * ROWS
                start = 0
                if first:
                    start = 2 * UNROLL
                    for i in range(-UNROLL, start):
                        step(i // UNROLL * UNROLL, i % UNROLL, par)
                with eng.Fori(0, (STATS_FROM - start) // UNROLL) as t:
                    for u in range(UNROLL):
                        step(t * UNROLL + g + start, u, par)
                with eng.Fori(0, GROUPS // UNROLL) as t:
                    for u in range(UNROLL):
                        step(t * UNROLL + g + STATS_FROM, u, par, None,
                             None if last else ("measure", g, t * UNROLL + u))
                for u in range(UNROLL):
                    step(g + (ROWS - UNROLL), u, par, ROWS - UNROLL + u, None if last else ("finish", img + 1))
                if last:
                    for u in range(UNROLL):
                        step(g + ROWS, u, par)

            run_image(0, 0, True, False)
            with eng.Fori(0, IMAGES // 2 - 1) as q:
                for s in range(2):
                    run_image(q * 2 + (1 + s), 1 - s, False, False)
            run_image(IMAGES - 1, (IMAGES - 1) % 2, False, True)

        def split(base, v):
            return base + v // UNROLL * UNROLL, v % UNROLL

        @block.tensor
        def _(pe):
            def x_transpose(base, v, par):
                g, m = split(base, v)
                pe.wait_ge(ring_in[m // 2], 4 * g + 16)
                if not known_below(base, 1 - v):
                    pe.wait_ge(xlo_done, base + v)
                for j in range(J):
                    mm = pe.transpose(xt_bank[:, j * P:(j + 1) * P], x_ring[:, m, j * C:(j + 1) * C], ident[:, :])
                mm.then_inc(xt_done, 1)

            def project_qk(base, v, par):
                pe.wait_ge(xlo_done, base + (v + 1))
                if not known_below(base, 1 - v):
                    pe.wait_ge(qklo_done, base + v)
                m = v % 2
                for t in range(2):
                    o = qk_bank[:, t * TOK:(t + 1) * TOK]
                    pe.matmul(o, w_lo[:, par, t, :], xc_hi[:, m, :], start=True, stop=False)
                    pe.matmul(o, w_hi[:, par, t, :], xc_lo[:, m, :], start=False, stop=False)
                    mm = pe.matmul(o, w_hi[:, par, t, :], xc_hi[:, m, :], start=False, stop=True)
                mm.then_inc(qk_done, 1)

            def project_v(base, v, par):
                if not known_below(base, 1 - v):
                    pe.wait_ge(vhi_done, base + v)
                m = v % 2
                for j in range(J):
                    o = v_bank[:, j * C:(j + 1) * C]
                    c = slice(j * P, (j + 1) * P)
                    pe.matmul(o, xc_lo[:, m, c], w_hi[:, par, 2, :], start=True, stop=False)
                    pe.matmul(o, xc_hi[:, m, c], w_lo[:, par, 2, :], start=False, stop=False)
                    mm = pe.matmul(o, xc_hi[:, m, c], w_hi[:, par, 2, :], start=False, stop=True)
                mm.then_inc(v_done, 1)

            def scores(base, v, par):
                pe.wait_ge(qklo_done, base + (v + 1))
                if not known_below(base, 1 - v):
                    for h in range(HEADS):
                        pe.wait_ge(exp_done[h], base + v)
                m = v % 2
                for a in range(J):
                    for n, (q, k) in enumerate(((qk_lo, qk_hi), (qk_hi, qk_lo), (qk_hi, qk_hi))):
                        for h in range(HEADS):
                            c = slice(h * HC, (h + 1) * HC)
                            mm = pe.matmul(s_bank[h][:, a * TOK:(a + 1) * TOK], q[c, m, 0, a * P:(a + 1) * P],
                                           k[c, m, 1, :], start=(n == 0), stop=(n == 2))
                mm.then_inc(s_done, 1)

            def p_transpose(h, base, v, par):
                pe.wait_ge(exp_done[h], base + (v + 1))
                if not known_below(base, 1 - v):
                    pe.wait_ge(plo_done[h], base + v)
                for j in range(J):
                    for a in range(J):
                        mm = pe.transpose(t_bank[h][:, j * TOK + a * P:j * TOK + (a + 1) * P],
                                          prob[:, v % 2, h, a, j * P:(j + 1) * P], ident[:, :])
                mm.then_inc(t_done[h], 1)

            def values(base, v, par):
                pe.wait_ge(vlo_done, base + (v + 1))
                if not known_below(base, 1 - v):
                    pe.wait_ge(o_done, base + v)
                m = v % 2
                for h in range(HEADS):
                    pe.wait_ge(plo_done[h], base + (v + 1))
                    for a in range(J):
                        for j in range(J):
                            c = slice(j * TOK + a * P, j * TOK + (a + 1) * P)
                            for n, (pp, vv) in enumerate(((p_lo, v_hi), (p_hi, v_lo), (p_hi, v_hi))):
                                mm = pe.matmul(o_view[:, a * HEADS + h, :], pp[:, m, h, c], vv[:, v % 4, j, h, :],
                                               start=(j == 0 and n == 0), stop=(j == J - 1 and n == 2))
                mm.then_inc(pv_done, 1)

            def statistics(n, part):
                if part == 0:
                    pe.wait_ge(stat_step, n + 1)
                    pe.matmul(xt_bank[:, 256:256 + GROUPS], mean_of[:, :], st[:, 0, :],
                              start=True, stop=True).then_inc(stat_mm, 1)
                elif part == 1:
                    pe.wait_ge(stat_step, n + 6)
                    pe.matmul(xt_bank[:, 256:256 + GROUPS], var_of[:, :], st[:, 3, :],
                              start=True, stop=True).then_inc(stat_mm, 1)
                else:
                    pe.wait_ge(stat_step, n + 20)
                    for i in range(2):
                        mm = pe.transpose(xt_bank[:, 256 + i * P:256 + (i + 1) * P],
                                          wide[:, i, :, :].rearrange("p g c -> p (g c)"), ident[:, :])
                    mm.then_inc(stat_mm, 1)

            pe.wait_ge(const_done, 12)
            pe.wait_ge(setup_dve, 9)
            for t in range(3):
                pe.transpose(s_bank[0][:, t * P:(t + 1) * P], w_in[:, t, :], ident[:, :])
            for i in range(2):
                mm = pe.transpose(s_bank[1][:, i * P:(i + 1) * P], spread[:, i, :], ident[:, :])
            mm.then_inc(setup_pe, 1)
            for part in range(3):
                statistics(0, part)
            pe.wait_ge(stat_step, STAT_STEPS)

            def share(base, u, par, what):
                if what[0] == "finish":
                    if u < 3:
                        pe.wait_ge(xlo_done, base + (u + 2))
                        statistics(what[1] * STAT_STEPS, u)
                    pe.wait_ge(stat_step, what[1] * STAT_STEPS + (2, 8, 21, STAT_STEPS)[u])

            def order(run, measuring):
                measuring()
                run(-1, p_transpose, 0)
                run(+2, x_transpose)
                run(0, scores)
                run(+1, project_qk)
                run(+1, project_v)
                run(-2, values)
                run(-1, p_transpose, 1)

            schedule(pe, order, share)

        @block.scalar
        def _(act):
            def x_high(base, v, par):
                m = v % 2
                act.wait_ge(xt_done, base + (v + 1))
                if not known_below(base, 2 - v):
                    act.wait_ge(v_done, base + (v - 1))
                act.activation(xc_hi[:, m, :], xt_bank[:, 0:TOK], ACT.Identity,
                               bias=norm[:, par, 0:1]).then_inc(xhi_done, 1)

            def qk_high(base, v, par):
                m = v % 2
                act.wait_ge(qk_done, base + (v + 1))
                if not known_below(base, 2 - v):
                    act.wait_ge(s_done, base + (v - 1))
                for t in range(2):
                    ins = act.activation(qk_hi[:, m, t, :], qk_bank[:, t * TOK:(t + 1) * TOK], ACT.Identity,
                                         bias=b_in[:, t:t + 1])
                ins.then_inc(qkhi_done, 1)

            def v_high(base, v, par):
                act.wait_ge(v_done, base + (v + 1))
                if not known_below(base, 4 - v):
                    act.wait_ge(pv_done, base + (v - 3))
                bank_view = v_bank[:, 0:J * C].rearrange("p (j h c) -> p j h c", j=J, h=HEADS)
                if not known_below(base, 2 - v):
                    act.wait_ge(vlo_done, base + (v - 1))
                act.activation(v_full[:, v % 2, :, :, :], bank_view, ACT.Copy)
                act.activation(v_hi[:, v % 4, :, :, 0:HC], bank_view, ACT.Copy).then_inc(vhi_done, 1)

            def exponent(h, base, v, par):
                m = v % 2
                act.wait_ge(max_done[h], base + (v + 1))
                if not known_below(base, 2 - v):
                    act.wait_ge(t_done[h], base + (v - 1))
                for a in range(J):
                    ins = act.activation(prob[:, m, h, a, :], s_bank[h][:, a * TOK:(a + 1) * TOK], ACT.Exp,
                                         bias=neg_max[:, m, h, a:a + 1])
                ins.then_inc(exp_done[h], 1)

            def p_high(h, base, v, par):
                act.wait_ge(t_done[h], base + (v + 1))
                if not known_below(base, 2 - v):
                    act.wait_ge(pv_done, base + (v - 1))
                act.activation(p_hi[:, v % 2, h, :], t_bank[h][:, :], ACT.Copy,
                               scale=P_SCALE).then_inc(phi_done[h], 1)

            act.wait_ge(setup_dve, 13)
            def order(run, measuring):
                run(-2, p_high, 1)
                run(+2, x_high)
                run(0, v_high)
                run(-1, p_high, 0)
                run(+1, qk_high)
                run(0, exponent, 0)
                run(0, exponent, 1)

            schedule(act, order)

        @block.vector
        def _(dve):
            def x_low(base, v, par):
                m = v % 2
                dve.wait_ge(xhi_done, base + (v + 1))
                dve.scalar_tensor_tensor(out=xc_lo[:, m, :], in0=xt_bank[:, 0:TOK], scalar=norm[:, par, 0:1],
                                         in1=xc_hi[:, m, :].bitcast(F32), op0=ALU.add,
                                         op1=ALU.subtract).then_inc(xlo_done, 1)

            def qk_low(base, v, par):
                m = v % 2
                dve.wait_ge(qkhi_done, base + (v + 1))
                for t in range(2):
                    ins = dve.scalar_tensor_tensor(out=qk_lo[:, m, t, :], in0=qk_bank[:, t * TOK:(t + 1) * TOK],
                                                   scalar=b_in[:, t:t + 1], in1=qk_hi[:, m, t, :].bitcast(F32),
                                                   op0=ALU.add, op1=ALU.subtract)
                ins.then_inc(qklo_done, 1)

            def row_max(h, base, v, par):
                m = v % 2
                dve.wait_ge(s_done, base + (v + 1))
                dve.tensor_reduce(neg_max[:, m, h, :], s_bank[h][:, :].rearrange("p (a k) -> p a k", a=J),
                                  AX.X, ALU.max, negate=True).then_inc(max_done[h], 1)

            def p_low(h, base, v, par):
                dve.wait_ge(phi_done[h], base + (v + 1))
                dve.scalar_tensor_tensor(out=p_lo[:, v % 2, h, :], in0=t_bank[h][:, :], scalar=P_SCALE,
                                         in1=p_hi[:, v % 2, h, :], op0=ALU.mult,
                                         op1=ALU.subtract).then_inc(plo_done[h], 1)

            def sums(base, v, par):
                dve.wait_ge(pv_done, base + (v + 1))
                dve.reciprocal(rsum[:, v % 2, :], o_view[:, :, HC]).then_inc(rsum_done, 1)

            def divide(base, v, par):
                m = v % 2
                dve.wait_ge(rsum_done, base + (v + 1))
                if not known_below(base, 2 - v):
                    dve.wait_ge(back_done, base + (v - 1))
                dve.tensor_tensor(o_norm[:, m, :, :], o_view[:, :, 0:HC],
                                  rsum[:, m, :].unsqueeze(2).broadcast_to([P, J * HEADS, HC]),
                                  ALU.mult).then_inc(o_done, 1)

            def measure(group, par):
                dve.bn_stats(bn[:, bass.ds(group, 1), :, :].rearrange("p g a b -> p (g a b)"),
                             image[:, par, :, :].rearrange("p r (j c) -> p (r j) c", j=J)[:, :, bass.ds(group * GC, GC)]
                             ).then_inc(bn_done, 1)

            def statistics(n, images, par, part):
                at = [n + (0, 2, 8, 21)[part]]

                def chain(ins):
                    at[0] = at[0] + 1
                    ins.then_inc(stat_step, 1)
                    dve.wait_ge(stat_step, at[0])

                if part == 0:
                    dve.wait_ge(bn_done, (images + 1) * GROUPS)
                    chain(dve.tensor_tensor(st[:, 0, :], bn[:, :, 0, 1], bn[:, :, 1, 1], ALU.add))
                    dve.wait_ge(stat_mm, images * 3 + 1)
                    chain(dve.tensor_copy(st[:, 1, :], xt_bank[:, 256:256 + GROUPS]))
                elif part == 1:
                    chain(dve.tensor_tensor(dev[:, :, :], bn[:, :, :, 1],
                                            st[:, 1, :].unsqueeze(2).broadcast_to([P, GROUPS, 2]), ALU.subtract))
                    chain(dve.tensor_tensor(dev[:, :, :], dev[:, :, :], dev[:, :, :], ALU.mult))
                    chain(dve.scalar_tensor_tensor(out=dev[:, :, :], in0=dev[:, :, :], scalar=float(HALF_COUNT),
                                                   in1=bn[:, :, :, 2], op0=ALU.mult, op1=ALU.add))
                    chain(dve.tensor_tensor(st[:, 3, :], dev[:, :, 0], dev[:, :, 1], ALU.add))
                    chain(dve.tensor_scalar(wide[:, 0, :, :], st[:, 1, :].unsqueeze(2).broadcast_to([P, GROUPS, GC]),
                                            -1.0, None, ALU.mult))
                    dve.wait_ge(stat_mm, images * 3 + 2)
                    chain(dve.tensor_scalar(st[:, 4, :], xt_bank[:, 256:256 + GROUPS], EPS, None, ALU.add))
                elif part == 2:
                    chain(dve.tensor_scalar(st[:, 2, :].bitcast(I32), st[:, 4, :].bitcast(I32), 1, None,
                                            ALU.logical_shift_right))
                    chain(dve.tensor_scalar(st[:, 5, :].bitcast(I32), st[:, 2, :].bitcast(I32), -1.0,
                                            float(0x5F3759DF), ALU.mult, ALU.add))
                    for _ in range(3):
                        chain(dve.tensor_tensor(st[:, 2, :], st[:, 5, :], st[:, 5, :], ALU.mult))
                        chain(dve.scalar_tensor_tensor(out=st[:, 2, :], in0=st[:, 2, :], scalar=-0.5,
                                                       in1=st[:, 4, :], op0=ALU.mult, op1=ALU.mult))
                        chain(dve.scalar_tensor_tensor(out=st[:, 5, :], in0=st[:, 2, :], scalar=1.5,
                                                       in1=st[:, 5, :], op0=ALU.add, op1=ALU.mult))
                    chain(dve.tensor_copy(wide[:, 1, :, :],
                                          st[:, 5, :].unsqueeze(2).broadcast_to([P, GROUPS, GC])))
                    dve.wait_ge(stat_mm, images * 3 + 3)
                    chain(dve.tensor_copy(norm[:, par, :],
                                          xt_bank[:, 256:512].rearrange("p (i q) -> p i q", i=2)[:, :, 0]))
                else:
                    chain(dve.tensor_scalar(w_norm[:, :, :], w_t[:, :, :], norm[:, par, 1:2], None, ALU.mult))
                    chain(dve.tensor_copy(w_hi[:, par, :, :], w_norm[:, :, :]))
                    chain(dve.tensor_tensor(w_lo[:, par, :, :], w_norm[:, :, :], w_hi[:, par, :, :].bitcast(F32),
                                            ALU.subtract))

            n = [0]

            def chain(ins):
                n[0] += 1
                ins.then_inc(setup_dve, 1)
                dve.wait_ge(setup_dve, n[0])

            dve.wait_ge(w_loaded, 64)
            dve.tensor_reduce(v_bound[:, 0:1], w_in[:, 2, :], AX.X, ALU.add, apply_absolute_value=True)\
                .then_inc(setup_dve, 1)
            n[0] += 1
            chain(dve.tensor_scalar(w_in[:, 0, :], w_in[:, 0, :], SCALE, None, ALU.mult))
            chain(dve.tensor_scalar(v_bound[:, 1:2], v_bound[:, 0:1], math.sqrt(NORM_COUNT), 2.0 ** -60,
                                    ALU.mult, ALU.max))
            chain(dve.tensor_scalar(v_bound[:, 2:3].bitcast(I32), v_bound[:, 1:2].bitcast(I32), 0x7F800000, None,
                                    ALU.bitwise_and))
            chain(dve.tensor_scalar(v_bound[:, 2:3], v_bound[:, 2:3], 1.0 / V_TOP, None, ALU.mult))
            chain(dve.reciprocal(v_bound[:, 3:4], v_bound[:, 2:3]))
            chain(dve.tensor_scalar(w_in[:, 2, :], w_in[:, 2, :], v_bound[:, 3:4], None, ALU.mult))
            dve.wait_ge(const_done, 4)
            chain(dve.tensor_scalar(spread[:, 0, :], mean_of[:, :], 0.0, v_bound[:, 2:3], ALU.mult, ALU.add))
            chain(dve.tensor_scalar(spread[:, 1, :], mean_of[:, :], 0.0, b_in[:, 2:3], ALU.mult, ALU.add))
            dve.wait_ge(setup_pe, 1)
            chain(dve.tensor_copy(w_t[:, :, :], s_bank[0][:, 0:3 * P].rearrange("p (t c) -> p t c", t=3)))
            for j in range(J):
                chain(dve.tensor_copy(v_back[:, j, :], s_bank[1][:, 0:P]))
            dve.tensor_scalar(b_in[:, 0:1], b_in[:, 0:1], SCALE, None, ALU.mult).then_inc(setup_dve, 1)
            n[0] += 1
            for j in range(J):
                chain(dve.tensor_copy(v_bias[:, j, :], s_bank[1][:, P:2 * P]))
            assert n[0] == 15

            dve.wait_ge(loaded[0], 16 * LOADS)
            for group in range(GROUPS):
                measure(group, 0)
            for part in range(4):
                statistics(0, 0, 0, part)

            def share(base, u, par, what):
                if what[0] == "measure":
                    if u == 0:
                        dve.wait_ge(loaded[1 - par], (what[1] + ROWS * par) * (16 * LOADS // (2 * ROWS)) + 16 * LOADS)
                    measure(what[2], 1 - par)
                else:
                    statistics(what[1] * STAT_STEPS, what[1], 1 - par, u)

            def order(run, measuring):
                measuring()
                run(-3, divide)
                run(-2, p_low, 1)
                run(+2, x_low)
                run(0, row_max, 1)
                run(0, row_max, 0)
                run(-1, p_low, 0)
                run(+1, qk_low)
                run(-2, sums)

            schedule(dve, order, share)

        @block.gpsimd
        def _(pool):
            def v_low(base, v, par):
                m = v % 2
                pool.wait_ge(vhi_done, base + (v + 1))
                pool.tensor_tensor(v_lo[:, v % 4, :, :, 0:HC], v_full[:, m, :, :, :], v_hi[:, v % 4, :, :, 0:HC],
                                   ALU.subtract).then_inc(vlo_done, 1)

            def add_bias(base, v, par):
                g, m = split(base, v)
                pool.wait_ge(ring_in[m // 2], 4 * g + 16)
                if not known_below(base, 4 - v):
                    pool.wait_ge(y_done, base + (v - 3))
                pool.tensor_tensor(xb_ring[:, m, :], x_ring[:, m, :],
                                   v_bias[:, :, :].rearrange("p j c -> p (j c)"), ALU.add).then_inc(xb_done, 1)

            def finish(base, v, par):
                g, m = split(base, v)
                pool.wait_ge(o_done, base + (v + 1))
                pool.tensor_tensor(o_back[:, v % 2, :], o_norm[:, v % 2, :, :].rearrange("p a c -> p (a c)"),
                                   v_back[:, :, :].rearrange("p j c -> p (j c)"), ALU.mult).then_inc(back_done, 1)
                pool.wait_ge(back_done, base + (v + 1))
                pool.wait_ge(xb_done, base + (v + 1))
                if not known_below(base, 4 - v):
                    pool.wait_ge(stored[m // 2], 4 * g)
                pool.tensor_tensor(y_ring[:, m, :], xb_ring[:, m, :], o_back[:, v % 2, :],
                                   ALU.add).then_inc(y_done, 1)

            pool.memset(ident[:, :], 0.0).then_inc(const_done, 1)
            pool.memset(mean_of[:, :], 1.0 / (2 * P)).then_inc(const_done, 1)
            pool.memset(var_of[:, :], 1.0 / NORM_COUNT).then_inc(const_done, 1)
            pool.wait_ge(const_done, 3)
            pool.affine_select(out=ident[:, :], in_=ident[:, :], compare_op=ALU.not_equal, fill=1.0, base=0,
                               pattern=[[-1, P]], channel_multiplier=1).then_inc(const_done, 1)
            for m in range(4):
                pool.memset(v_hi[:, m, :, :, HC:HC + 1], 1.0).then_inc(const_done, 1)
                pool.memset(v_lo[:, m, :, :, HC:HC + 1], 0.0).then_inc(const_done, 1)
            pool.wait_ge(setup_dve, 15)
            def order(run, measuring):
                run(0, add_bias)
                run(-3, finish)
                run(0, v_low)

            schedule(pool, order)


_INS = ["x", "L0_conv_W_qkv", "L0_conv_b_qkv"]


def kernel(**inputs):
    import numpy as _np
    import concourse.bacc as _bacc
    from concourse import mybir as _mybir
    from concourse.bass_utils import run_bass_kernel_spmd as _run

    nc = _bacc.Bacc("TRN2", target_bir_lowering=False, num_devices=1)
    arrays, args = {}, []
    for name in _INS:
        a = _np.ascontiguousarray(inputs[name])
        arrays[f"in_{name}_dram"] = a
        args.append(nc.dram_tensor(f"in_{name}_dram", a.shape, _mybir.dt.from_np(a.dtype), kind="ExternalInput").ap())
    shape = inputs["x"].shape
    args.append(nc.dram_tensor("out_0_dram", shape, _mybir.dt.float32, kind="ExternalOutput").ap())
    groupnorm_attention(nc, *args)
    r = _run(nc, [arrays], core_ids=[0])
    return r.results[0]["out_0_dram"]
```

```python
import math
from contextlib import ExitStack

import concourse.bass as bass
from concourse import mybir

F32 = mybir.dt.float32
F32R = mybir.dt.float32r
F16 = mybir.dt.float16
I32 = mybir.dt.int32
ALU = mybir.AluOpType
ACT = mybir.ActivationFunctionType
AX = mybir.AxisListType

P = 128
UNROLL = 4
P_SCALE = 2.0 ** 15
V_TOP = 2.0 ** 14
EPS = 1e-5


def groupnorm_attention(nc: bass.Bass, x: bass.AP, w: bass.AP, b: bass.AP, out: bass.AP):
    IMAGES, ROWS, TOK, C = x.shape
    HEADS, GROUPS = 2, 32
    HC = C // HEADS
    GC = C // GROUPS
    J = TOK // P
    BLOCKS = IMAGES * ROWS
    LAST = BLOCKS - 1
    SCALE = 1.0 / math.sqrt(C)
    NORM_COUNT = ROWS * TOK * GC
    HALF_COUNT = ROWS * J * GC // 2
    assert C == P and J == 2 and ROWS * J * GC == 512 and BLOCKS % UNROLL == 0
    PAIRS = ROWS // 2
    FINISH = 12
    STATS_FROM = ROWS - FINISH - GROUPS
    assert STATS_FROM % UNROLL == 0 and FINISH % UNROLL == 0
    X_AHEAD = 2
    MEASURE = "measure"
    LOADS = 4
    assert LOADS * UNROLL <= STATS_FROM
    LB = ROWS // LOADS

    x_img = x.rearrange("n r (p j) c -> n p r (j c)", j=J)
    out_pairs = out.rearrange("n (k r) (p j) c -> (n k) p r (j c)", r=2, j=J)

    with ExitStack() as ctx:
        def sb(name, shape, dt=F32):
            return ctx.enter_context(nc.sbuf_tensor(name, shape, dt))

        def bank(name):
            return ctx.enter_context(nc.psum_tensor(name, [P, 512], F32))

        def sem(name):
            return ctx.enter_context(nc.semaphore(name))

        image = sb("image", [P, 2, ROWS, J * C])
        x_ring = sb("x_ring", [P, 4, J * C])
        xb_ring = sb("xb_ring", [P, 4, J * C])
        y_ring = sb("y_ring", [P, 4, J * C])
        xc_hi = sb("xc_hi", [P, 2, TOK], F32R)
        xc_lo = sb("xc_lo", [P, 2, TOK], F32R)
        qk_hi = sb("qk_hi", [P, 2, 2, TOK], F32R)
        qk_lo = sb("qk_lo", [P, 2, 2, TOK], F32R)
        prob = sb("prob", [P, 2, HEADS, J, TOK])
        p_hi = sb("p_hi", [P, 2, HEADS, J * TOK], F16)
        p_lo = sb("p_lo", [P, 2, HEADS, J * TOK], F16)
        v_full = sb("v_full", [P, 2, J, HEADS, HC])
        v_hi = sb("v_hi", [P, 4, J, HEADS, HC + 1], F16)
        v_lo = sb("v_lo", [P, 4, J, HEADS, HC + 1], F16)
        neg_max = sb("neg_max", [P, 2, HEADS, J])
        rsum = sb("rsum", [P, 2, J * HEADS])
        o_norm = sb("o_norm", [P, 2, J * HEADS, HC])
        o_back = sb("o_back", [P, 2, J * HEADS * HC])

        ident = sb("ident", [P, P])
        w_in = sb("w_in", [P, 3, C])
        b_in = sb("b_in", [P, 3])
        w_t = sb("w_t", [P, 3, C])
        w_norm = sb("w_norm", [P, 3, C])
        w_hi = sb("w_hi", [P, 2, 3, C], F32R)
        w_lo = sb("w_lo", [P, 2, 3, C], F32R)
        v_bound = sb("v_bound", [P, 4])
        spread = sb("spread", [P, 2, P])
        v_back = sb("v_back", [P, J, C])
        v_bias = sb("v_bias", [P, J, C])

        bn = sb("bn", [P, GROUPS, 2, 3])
        first_bn = sb("first_bn", [P, GROUPS, 2 * LOADS, 3])
        first_dev = sb("first_dev", [P, GROUPS, 2 * LOADS])
        st = sb("st", [P, 6, GROUPS])
        dev = sb("dev", [P, GROUPS, 2])
        wide = sb("wide", [P, 2, GROUPS, GC])
        norm = sb("norm", [P, 2, 2])
        mean_of = sb("mean_of", [P, P])
        var_of = sb("var_of", [P, P])

        xt_bank = bank("xt_bank")
        qk_bank = bank("qk_bank")
        v_bank = bank("v_bank")
        s_bank = [bank(f"s_bank{h}") for h in range(HEADS)]
        t_bank = [bank(f"t_bank{h}") for h in range(HEADS)]
        o_bank = bank("o_bank")
        o_view = o_bank[:, 0:J * HEADS * (HC + 1)].rearrange("p (a c) -> p a c", c=HC + 1)

        first_in = [sem(f"first_in{i}") for i in range(LOADS)]
        loaded = [sem(f"loaded{i}") for i in range(2)]
        ring_in = [sem(f"ring_in{i}") for i in range(2)]
        stored = [sem(f"stored{i}") for i in range(2)]
        xt_done = sem("xt_done")
        xhi_done = sem("xhi_done")
        xlo_done = sem("xlo_done")
        xb_done = sem("xb_done")
        qk_done = sem("qk_done")
        qkhi_done = sem("qkhi_done")
        qklo_done = sem("qklo_done")
        v_done = sem("v_done")
        vhi_done = sem("vhi_done")
        vlo_done = sem("vlo_done")
        s_done = sem("s_done")
        max_done = [sem(f"max_done{h}") for h in range(HEADS)]
        exp_done = [sem(f"exp_done{h}") for h in range(HEADS)]
        t_done = [sem(f"t_done{h}") for h in range(HEADS)]
        phi_done = [sem(f"phi_done{h}") for h in range(HEADS)]
        plo_done = [sem(f"plo_done{h}") for h in range(HEADS)]
        pv_done = sem("pv_done")
        rsum_done = sem("rsum_done")
        o_done = sem("o_done")
        back_done = sem("back_done")
        y_done = sem("y_done")
        bn_done = sem("bn_done")
        stat_step = sem("stat_step")
        stat_mm = sem("stat_mm")
        w_loaded = sem("w_loaded")
        const_done = sem("const_done")
        setup_dve = sem("setup_dve")
        setup_pe = sem("setup_pe")

        STAT_STEPS = 25
        MEANS_READY, SQUARES_READY, RSTD_READY = 1, 7, 21
        STAT_AT = J * HEADS * (HC + 1)
        STAT_MM_AT = (0, 2, 6)
        STAT_OPS_AT = {0: ((1,),), 1: ((2,), (3,), (4,), (5,)), 2: ((6,), (7,)), 3: ((8, 9), (10,), (11,), (12,)),
                       4: ((13,), (14,), (15,), (16,)), 5: ((17,), (18,), (19,), (20,)), 6: ((21,),),
                       7: ((22,), (23,), (24,), (25,))}

        block = ctx.enter_context(nc.Block())

        def known_below(base, n):
            return isinstance(base, int) and base < n

        @block.sync
        def _(sp):
            def load_image(img, part, parity):
                rows = bass.ds(part * LB, LB)
                sp.dma_start(image[:, parity, rows, :], x_img[img, :, rows, :]).then_inc(loaded[parity], 16)

            def refill(g0, row0, parity, k):
                if not known_below(g0, UNROLL):
                    sp.wait_ge(xt_done, g0 + (2 * k + 2 - 4))
                    sp.wait_ge(xb_done, g0 + (2 * k + 2 - 4))
                sp.dma_start(x_ring[:, 2 * k:2 * k + 2, :],
                             image[:, parity, bass.ds(row0 + 2 * k, 2), :]).then_inc(ring_in[k], 16)

            def store(g0, pair0, k):
                sp.wait_ge(y_done, g0 + (2 * k + 2))
                sp.dma_start(out_pairs[bass.ds(pair0 + k, 1)].rearrange("a p r c -> (a p) r c"),
                             y_ring[:, 2 * k:2 * k + 2, :]).then_inc(stored[k], 16)

            sp.dma_start(w_in[:, :, :], w.rearrange("(t d) c -> d t c", d=P)).then_inc(w_loaded, 16)
            for t in range(3):
                sp.dma_start(b_in[:, t:t + 1], b[t * P:(t + 1) * P].rearrange("(d a) -> d a", a=1)).then_inc(w_loaded, 16)
            for part in range(LOADS):
                sp.dma_start(image[:, 0, part * LB:(part + 1) * LB, :],
                             x_img[0, :, part * LB:(part + 1) * LB, :]).then_inc(first_in[part], 16)

            def run_image(img, par, is_first, is_last):
                g = img * ROWS
                if is_first:
                    sp.wait_ge(first_in[0], 16)
                    assert 2 * UNROLL <= LB
                    refill(0, 0, par, 0)
                    refill(0, 0, par, 1)
                def loop(t):
                    for k in range(2):
                        refill(t * UNROLL + g + UNROLL, t * UNROLL + UNROLL, par, k)
                        if not known_below(t, 1) or not is_first:
                            store(t * UNROLL + g - UNROLL, t * 2 + img * PAIRS - 2, k)

                loop(0)
                start = 1
                if not is_last:
                    if not is_first:
                        for k in range(2):
                            sp.wait_ge(ring_in[k], 4 * g)
                    load_image(img + 1, 0, 1 - par)
                    with sp.Fori(start, LOADS) as t:
                        loop(t)
                        load_image(img + 1, t, 1 - par)
                    start = LOADS
                with sp.Fori(0, ROWS // UNROLL - 1 - start) as t:
                    loop(t + start)
                for k in range(2):
                    if not is_last:
                        refill(g + ROWS, 0, 1 - par, k)
                    store(g + (ROWS - 2 * UNROLL), img * PAIRS + (PAIRS - 4), k)
                if is_last:
                    for k in range(2):
                        store(g + (ROWS - UNROLL), img * PAIRS + (PAIRS - 2), k)

            run_image(0, 0, True, False)
            with sp.Fori(0, IMAGES // 2 - 1) as q:
                for s in range(2):
                    run_image(q * 2 + (1 + s), 1 - s, False, False)
            run_image(IMAGES - 1, (IMAGES - 1) % 2, False, True)
            for k in range(2):
                sp.wait_ge(stored[k], 16 * BLOCKS // 4)

        def schedule(eng, order, share=None):
            def step(base, u, par, row=None, what=None):
                def run(lead, stage, *head):
                    v = u + lead
                    if isinstance(base, int) and not 0 <= base + v <= LAST:
                        return
                    stage(*head, base, v, par if row is None or 0 <= row + lead < ROWS else 1 - par)

                def next_image(place):
                    if what is not None and (place == MEASURE) == (what[0] == MEASURE):
                        share(base, u, par, what, place)

                order(run, next_image)

            def run_image(img, par, first, last):
                g = img * ROWS
                start = 0
                if first:
                    start = 2 * UNROLL
                    for i in range(-UNROLL, start):
                        step(i // UNROLL * UNROLL, i % UNROLL, par)
                with eng.Fori(0, (STATS_FROM - start) // UNROLL) as t:
                    for u in range(UNROLL):
                        step(t * UNROLL + g + start, u, par)
                with eng.Fori(0, GROUPS // UNROLL) as t:
                    for u in range(UNROLL):
                        step(t * UNROLL + g + STATS_FROM, u, par, None,
                             None if last else (MEASURE, img + 1, t * UNROLL + u))
                for i in range(FINISH):
                    row = ROWS - FINISH + i
                    step(g + row // UNROLL * UNROLL, row % UNROLL, par, row, None if last else ("finish", img + 1, i))
                if last:
                    for u in range(UNROLL):
                        step(g + ROWS, u, par)

            run_image(0, 0, True, False)
            with eng.Fori(0, IMAGES // 2 - 1) as q:
                for s in range(2):
                    run_image(q * 2 + (1 + s), 1 - s, False, False)
            run_image(IMAGES - 1, (IMAGES - 1) % 2, False, True)

        def split(base, v):
            return base + v // UNROLL * UNROLL, v % UNROLL

        @block.tensor
        def _(pe):
            def x_transpose(base, v, par):
                g, m = split(base, v)
                pe.wait_ge(ring_in[m // 2], 4 * g + 16)
                if not known_below(base, 1 - v):
                    pe.wait_ge(xlo_done, base + v)
                for j in range(J):
                    mm = pe.transpose(xt_bank[:, j * P:(j + 1) * P], x_ring[:, m, j * C:(j + 1) * C], ident[:, :])
                mm.then_inc(xt_done, 1)

            def project_qk(base, v, par):
                pe.wait_ge(xlo_done, base + (v + 1))
                if not known_below(base, 1 - v):
                    pe.wait_ge(qklo_done, base + v)
                m = v % 2
                for t in range(2):
                    o = qk_bank[:, t * TOK:(t + 1) * TOK]
                    pe.matmul(o, w_lo[:, par, t, :], xc_hi[:, m, :], start=True, stop=False)
                    pe.matmul(o, w_hi[:, par, t, :], xc_lo[:, m, :], start=False, stop=False)
                    mm = pe.matmul(o, w_hi[:, par, t, :], xc_hi[:, m, :], start=False, stop=True)
                mm.then_inc(qk_done, 1)

            def project_v(base, v, par):
                if not known_below(base, 1 - v):
                    pe.wait_ge(vhi_done, base + v)
                m = v % 2
                for j in range(J):
                    o = v_bank[:, j * C:(j + 1) * C]
                    c = slice(j * P, (j + 1) * P)
                    pe.matmul(o, xc_lo[:, m, c], w_hi[:, par, 2, :], start=True, stop=False)
                    pe.matmul(o, xc_hi[:, m, c], w_lo[:, par, 2, :], start=False, stop=False)
                    mm = pe.matmul(o, xc_hi[:, m, c], w_hi[:, par, 2, :], start=False, stop=True)
                mm.then_inc(v_done, 1)

            def scores(base, v, par):
                pe.wait_ge(qklo_done, base + (v + 1))
                if not known_below(base, 1 - v):
                    for h in range(HEADS):
                        pe.wait_ge(exp_done[h], base + v)
                m = v % 2
                for a in range(J):
                    for n, (q, k) in enumerate(((qk_lo, qk_hi), (qk_hi, qk_lo), (qk_hi, qk_hi))):
                        for h in range(HEADS):
                            c = slice(h * HC, (h + 1) * HC)
                            mm = pe.matmul(s_bank[h][:, a * TOK:(a + 1) * TOK], q[c, m, 0, a * P:(a + 1) * P],
                                           k[c, m, 1, :], start=(n == 0), stop=(n == 2))
                mm.then_inc(s_done, 1)

            def p_transpose(h, base, v, par):
                pe.wait_ge(exp_done[h], base + (v + 1))
                if not known_below(base, 1 - v):
                    pe.wait_ge(plo_done[h], base + v)
                for j in range(J):
                    for a in range(J):
                        mm = pe.transpose(t_bank[h][:, j * TOK + a * P:j * TOK + (a + 1) * P],
                                          prob[:, v % 2, h, a, j * P:(j + 1) * P], ident[:, :])
                mm.then_inc(t_done[h], 1)

            def values(base, v, par):
                pe.wait_ge(vlo_done, base + (v + 1))
                if not known_below(base, 1 - v):
                    pe.wait_ge(o_done, base + v)
                m = v % 2
                for h in range(HEADS):
                    pe.wait_ge(plo_done[h], base + (v + 1))
                    for a in range(J):
                        for j in range(J):
                            c = slice(j * TOK + a * P, j * TOK + (a + 1) * P)
                            for n, (pp, vv) in enumerate(((p_lo, v_hi), (p_hi, v_lo), (p_hi, v_hi))):
                                mm = pe.matmul(o_view[:, a * HEADS + h, :], pp[:, m, h, c], vv[:, v % 4, j, h, :],
                                               start=(j == 0 and n == 0), stop=(j == J - 1 and n == 2))
                mm.then_inc(pv_done, 1)

            def statistics(n, part):
                if part == 0:
                    pe.wait_ge(stat_step, n + MEANS_READY)
                    pe.matmul(o_bank[:, STAT_AT:STAT_AT + GROUPS], mean_of[:, :], st[:, 0, :],
                              start=True, stop=True).then_inc(stat_mm, 1)
                elif part == 1:
                    pe.wait_ge(stat_step, n + SQUARES_READY)
                    pe.matmul(o_bank[:, STAT_AT:STAT_AT + GROUPS], var_of[:, :], st[:, 3, :], start=True, stop=True)
                    pe.transpose(o_bank[:, STAT_AT + GROUPS:STAT_AT + GROUPS + P],
                                 wide[:, 0, :, :].rearrange("p g c -> p (g c)"), ident[:, :]).then_inc(stat_mm, 1)
                else:
                    pe.wait_ge(stat_step, n + RSTD_READY)
                    pe.transpose(o_bank[:, STAT_AT:STAT_AT + P],
                                 wide[:, 1, :, :].rearrange("p g c -> p (g c)"), ident[:, :]).then_inc(stat_mm, 1)

            pe.wait_ge(const_done, 12)
            pe.wait_ge(setup_dve, 9)
            for t in range(3):
                pe.transpose(s_bank[0][:, t * P:(t + 1) * P], w_in[:, t, :], ident[:, :])
            for i in range(2):
                mm = pe.transpose(s_bank[1][:, i * P:(i + 1) * P], spread[:, i, :], ident[:, :])
            mm.then_inc(setup_pe, 1)
            for part in range(3):
                statistics(0, part)
            pe.wait_ge(stat_step, STAT_STEPS)

            def share(base, u, par, what, pos):
                if what[2] in STAT_MM_AT:
                    pe.wait_ge(o_done, base + (u - 2))
                    statistics(what[1] * STAT_STEPS, STAT_MM_AT.index(what[2]))

            def order(run, next_image):
                run(+1, project_qk)
                run(-1, p_transpose, 0)
                run(0, scores)
                run(-1, p_transpose, 1)
                run(+1, project_v)
                next_image(0)
                run(-2, values)
                run(+3, x_transpose)

            schedule(pe, order, share)

        @block.scalar
        def _(act):
            def x_high(base, v, par):
                m = v % 2
                act.wait_ge(xt_done, base + (v + 1))
                if not known_below(base, 2 - v):
                    act.wait_ge(v_done, base + (v - 1))
                act.activation(xc_hi[:, m, :], xt_bank[:, 0:TOK], ACT.Identity,
                               bias=norm[:, par, 0:1]).then_inc(xhi_done, 1)

            def qk_high(base, v, par):
                m = v % 2
                act.wait_ge(qk_done, base + (v + 1))
                if not known_below(base, 2 - v):
                    act.wait_ge(s_done, base + (v - 1))
                for t in range(2):
                    ins = act.activation(qk_hi[:, m, t, :], qk_bank[:, t * TOK:(t + 1) * TOK], ACT.Identity,
                                         bias=b_in[:, t:t + 1])
                ins.then_inc(qkhi_done, 1)

            def v_high(base, v, par):
                act.wait_ge(v_done, base + (v + 1))
                if not known_below(base, 4 - v):
                    act.wait_ge(pv_done, base + (v - 3))
                bank_view = v_bank[:, 0:J * C].rearrange("p (j h c) -> p j h c", j=J, h=HEADS)
                if not known_below(base, 2 - v):
                    act.wait_ge(vlo_done, base + (v - 1))
                act.activation(v_full[:, v % 2, :, :, :], bank_view, ACT.Copy)
                act.activation(v_hi[:, v % 4, :, :, 0:HC], bank_view, ACT.Copy).then_inc(vhi_done, 1)

            def exponent(h, base, v, par):
                m = v % 2
                act.wait_ge(max_done[h], base + (v + 1))
                if not known_below(base, 2 - v):
                    act.wait_ge(t_done[h], base + (v - 1))
                for a in range(J):
                    ins = act.activation(prob[:, m, h, a, :], s_bank[h][:, a * TOK:(a + 1) * TOK], ACT.Exp,
                                         bias=neg_max[:, m, h, a:a + 1])
                ins.then_inc(exp_done[h], 1)

            def p_high(h, base, v, par):
                act.wait_ge(t_done[h], base + (v + 1))
                if not known_below(base, 2 - v):
                    act.wait_ge(pv_done, base + (v - 1))
                act.activation(p_hi[:, v % 2, h, :], t_bank[h][:, :], ACT.Copy,
                               scale=P_SCALE).then_inc(phi_done[h], 1)

            act.wait_ge(setup_dve, 13)
            def share(base, u, par, what, pos):
                if what[2] == FINISH - X_AHEAD:
                    act.wait_ge(stat_step, (what[1] + 1) * STAT_STEPS)

            def order(run, next_image):
                next_image(0)
                run(+2, x_high)
                run(+1, qk_high)
                run(0, v_high)
                run(-1, p_high, 0)
                run(-1, p_high, 1)
                run(0, exponent, 0)
                run(0, exponent, 1)

            schedule(act, order, share)

        @block.vector
        def _(dve):
            def x_low(base, v, par):
                m = v % 2
                dve.wait_ge(xhi_done, base + (v + 1))
                dve.scalar_tensor_tensor(out=xc_lo[:, m, :], in0=xt_bank[:, 0:TOK], scalar=norm[:, par, 0:1],
                                         in1=xc_hi[:, m, :].bitcast(F32), op0=ALU.add,
                                         op1=ALU.subtract).then_inc(xlo_done, 1)

            def qk_low(base, v, par):
                m = v % 2
                dve.wait_ge(qkhi_done, base + (v + 1))
                for t in range(2):
                    ins = dve.scalar_tensor_tensor(out=qk_lo[:, m, t, :], in0=qk_bank[:, t * TOK:(t + 1) * TOK],
                                                   scalar=b_in[:, t:t + 1], in1=qk_hi[:, m, t, :].bitcast(F32),
                                                   op0=ALU.add, op1=ALU.subtract)
                ins.then_inc(qklo_done, 1)

            def row_max(h, base, v, par):
                m = v % 2
                dve.wait_ge(s_done, base + (v + 1))
                dve.tensor_reduce(neg_max[:, m, h, :], s_bank[h][:, :].rearrange("p (a k) -> p a k", a=J),
                                  AX.X, ALU.max, negate=True).then_inc(max_done[h], 1)

            def p_low(h, base, v, par):
                dve.wait_ge(phi_done[h], base + (v + 1))
                dve.scalar_tensor_tensor(out=p_lo[:, v % 2, h, :], in0=t_bank[h][:, :], scalar=P_SCALE,
                                         in1=p_hi[:, v % 2, h, :], op0=ALU.mult,
                                         op1=ALU.subtract).then_inc(plo_done[h], 1)

            def sums(base, v, par):
                dve.wait_ge(pv_done, base + (v + 1))
                dve.reciprocal(rsum[:, v % 2, :], o_view[:, :, HC]).then_inc(rsum_done, 1)

            def divide(base, v, par):
                m = v % 2
                dve.wait_ge(rsum_done, base + (v + 1))
                if not known_below(base, 2 - v):
                    dve.wait_ge(back_done, base + (v - 1))
                dve.tensor_tensor(o_norm[:, m, :, :], o_view[:, :, 0:HC],
                                  rsum[:, m, :].unsqueeze(2).broadcast_to([P, J * HEADS, HC]),
                                  ALU.mult).then_inc(o_done, 1)

            def measure(group, par):
                dve.bn_stats(bn[:, bass.ds(group, 1), :, :].rearrange("p g a b -> p (g a b)"),
                             image[:, par, :, :].rearrange("p r (j c) -> p (r j) c", j=J)[:, :, bass.ds(group * GC, GC)]
                             ).then_inc(bn_done, 1)

            def measure_first(part, group):
                ins = dve.bn_stats(first_bn[:, group, 2 * part:2 * part + 2, :].rearrange("p a b -> p (a b)"),
                                   image[:, 0, part * LB:(part + 1) * LB, :].rearrange(
                                       "p r (j c) -> p (r j) c", j=J)[:, :, group * GC:(group + 1) * GC])
                if part == LOADS - 1:
                    ins.then_inc(bn_done, 1)

            def statistics(n, images, par, k, parts, bn, dev):
                if k > 1:
                    dve.wait_ge(stat_step, n + (k - 1))
                if k == 1:
                    dve.wait_ge(bn_done, (images + 1) * GROUPS)
                    ins = dve.tensor_reduce(st[:, 0, :], bn[:, :, :, 1], AX.X, ALU.add)
                elif k == 2:
                    dve.wait_ge(stat_mm, images * 3 + 1)
                    ins = dve.tensor_scalar(st[:, 1, :], o_bank[:, STAT_AT:STAT_AT + GROUPS], 2.0 / parts, None, ALU.mult)
                elif k == 3:
                    ins = dve.tensor_tensor(dev[:, :, :], bn[:, :, :, 1],
                                            st[:, 1, :].unsqueeze(2).broadcast_to([P, GROUPS, parts]), ALU.subtract)
                elif k == 4:
                    ins = dve.tensor_tensor(dev[:, :, :], dev[:, :, :], dev[:, :, :], ALU.mult)
                elif k == 5:
                    ins = dve.scalar_tensor_tensor(out=dev[:, :, :], in0=dev[:, :, :], scalar=HALF_COUNT * 2.0 / parts,
                                                   in1=bn[:, :, :, 2], op0=ALU.mult, op1=ALU.add)
                elif k == 6:
                    ins = dve.tensor_reduce(st[:, 3, :], dev[:, :, :], AX.X, ALU.add)
                elif k == 7:
                    ins = dve.tensor_scalar(wide[:, 0, :, :], st[:, 1, :].unsqueeze(2).broadcast_to([P, GROUPS, GC]),
                                            -1.0, None, ALU.mult)
                elif k == 8:
                    dve.wait_ge(stat_mm, images * 3 + 2)
                    ins = dve.tensor_scalar(st[:, 4, :], o_bank[:, STAT_AT:STAT_AT + GROUPS], EPS, None, ALU.add)
                elif k == 9:
                    ins = dve.tensor_copy(norm[:, par, 0:1], o_bank[:, STAT_AT + GROUPS:STAT_AT + GROUPS + 1])
                elif k == 10:
                    ins = dve.tensor_scalar(st[:, 2, :].bitcast(I32), st[:, 4, :].bitcast(I32), 1, None,
                                            ALU.logical_shift_right)
                elif k == 11:
                    ins = dve.tensor_scalar(st[:, 5, :].bitcast(I32), st[:, 2, :].bitcast(I32), -1.0,
                                            float(0x5F3759DF), ALU.mult, ALU.add)
                elif k in (12, 15, 18):
                    ins = dve.tensor_tensor(st[:, 2, :], st[:, 5, :], st[:, 5, :], ALU.mult)
                elif k in (13, 16, 19):
                    ins = dve.scalar_tensor_tensor(out=st[:, 2, :], in0=st[:, 2, :], scalar=-0.5,
                                                   in1=st[:, 4, :], op0=ALU.mult, op1=ALU.mult)
                elif k in (14, 17, 20):
                    ins = dve.scalar_tensor_tensor(out=st[:, 5, :], in0=st[:, 2, :], scalar=1.5,
                                                   in1=st[:, 5, :], op0=ALU.add, op1=ALU.mult)
                elif k == 21:
                    ins = dve.tensor_copy(wide[:, 1, :, :], st[:, 5, :].unsqueeze(2).broadcast_to([P, GROUPS, GC]))
                elif k == 22:
                    dve.wait_ge(stat_mm, images * 3 + 3)
                    ins = dve.tensor_copy(norm[:, par, 1:2], o_bank[:, STAT_AT:STAT_AT + 1])
                elif k == 23:
                    ins = dve.tensor_scalar(w_norm[:, :, :], w_t[:, :, :], norm[:, par, 1:2], None, ALU.mult)
                elif k == 24:
                    ins = dve.tensor_copy(w_hi[:, par, :, :], w_norm[:, :, :])
                else:
                    assert k == STAT_STEPS
                    ins = dve.tensor_tensor(w_lo[:, par, :, :], w_norm[:, :, :], w_hi[:, par, :, :].bitcast(F32),
                                            ALU.subtract)
                ins.then_inc(stat_step, 1)

            n = [0]

            def chain(ins):
                n[0] += 1
                ins.then_inc(setup_dve, 1)
                dve.wait_ge(setup_dve, n[0])

            dve.wait_ge(w_loaded, 64)
            dve.tensor_reduce(v_bound[:, 0:1], w_in[:, 2, :], AX.X, ALU.add, apply_absolute_value=True)\
                .then_inc(setup_dve, 1)
            n[0] += 1
            chain(dve.tensor_scalar(w_in[:, 0, :], w_in[:, 0, :], SCALE, None, ALU.mult))
            chain(dve.tensor_scalar(v_bound[:, 1:2], v_bound[:, 0:1], math.sqrt(NORM_COUNT), 2.0 ** -60,
                                    ALU.mult, ALU.max))
            chain(dve.tensor_scalar(v_bound[:, 2:3].bitcast(I32), v_bound[:, 1:2].bitcast(I32), 0x7F800000, None,
                                    ALU.bitwise_and))
            chain(dve.tensor_scalar(v_bound[:, 2:3], v_bound[:, 2:3], 1.0 / V_TOP, None, ALU.mult))
            chain(dve.reciprocal(v_bound[:, 3:4], v_bound[:, 2:3]))
            chain(dve.tensor_scalar(w_in[:, 2, :], w_in[:, 2, :], v_bound[:, 3:4], None, ALU.mult))
            dve.wait_ge(const_done, 4)
            chain(dve.tensor_scalar(spread[:, 0, :], mean_of[:, :], 0.0, v_bound[:, 2:3], ALU.mult, ALU.add))
            chain(dve.tensor_scalar(spread[:, 1, :], mean_of[:, :], 0.0, b_in[:, 2:3], ALU.mult, ALU.add))
            dve.wait_ge(setup_pe, 1)
            chain(dve.tensor_copy(w_t[:, :, :], s_bank[0][:, 0:3 * P].rearrange("p (t c) -> p t c", t=3)))
            for j in range(J):
                chain(dve.tensor_copy(v_back[:, j, :], s_bank[1][:, 0:P]))
            dve.tensor_scalar(b_in[:, 0:1], b_in[:, 0:1], SCALE, None, ALU.mult).then_inc(setup_dve, 1)
            n[0] += 1
            for j in range(J):
                chain(dve.tensor_copy(v_bias[:, j, :], s_bank[1][:, P:2 * P]))
            assert n[0] == 15

            for part in range(LOADS):
                dve.wait_ge(first_in[part], 16)
                for group in range(GROUPS):
                    measure_first(part, group)
            for k in range(1, STAT_STEPS + 1):
                statistics(0, 0, 0, k, 2 * LOADS, first_bn, first_dev)
            dve.wait_ge(stat_step, STAT_STEPS)

            def share(base, u, par, what, pos):
                if what[0] == MEASURE:
                    if u == 0:
                        dve.wait_ge(loaded[1 - par], (what[1] - 1 + par) * (8 * LOADS)
                                    + (1 - par) * (16 * LOADS))
                    measure(what[2], 1 - par)
                else:
                    ops = STAT_OPS_AT.get(what[2], ())
                    if pos < len(ops):
                        for k in ops[pos]:
                            statistics(what[1] * STAT_STEPS, what[1], 1 - par, k, 2, bn, dev)
                    elif pos == 0 and what[2] == FINISH - X_AHEAD:
                        dve.wait_ge(stat_step, (what[1] + 1) * STAT_STEPS)

            def order(run, next_image):
                next_image(0)
                run(-2, p_low, 1)
                next_image(1)
                run(+2, x_low)
                run(-3, divide)
                run(+1, qk_low)
                next_image(2)
                run(0, row_max, 0)
                run(0, row_max, 1)
                next_image(3)
                run(-1, p_low, 0)
                next_image(MEASURE)
                run(-2, sums)

            schedule(dve, order, share)

        @block.gpsimd
        def _(pool):
            def v_low(base, v, par):
                m = v % 2
                pool.wait_ge(vhi_done, base + (v + 1))
                pool.tensor_tensor(v_lo[:, v % 4, :, :, 0:HC], v_full[:, m, :, :, :], v_hi[:, v % 4, :, :, 0:HC],
                                   ALU.subtract).then_inc(vlo_done, 1)

            def add_bias(base, v, par):
                g, m = split(base, v)
                pool.wait_ge(ring_in[m // 2], 4 * g + 16)
                if not known_below(base, 4 - v):
                    pool.wait_ge(y_done, base + (v - 3))
                pool.tensor_tensor(xb_ring[:, m, :], x_ring[:, m, :],
                                   v_bias[:, :, :].rearrange("p j c -> p (j c)"), ALU.add).then_inc(xb_done, 1)

            def finish(base, v, par):
                g, m = split(base, v)
                pool.wait_ge(o_done, base + (v + 1))
                pool.tensor_tensor(o_back[:, v % 2, :], o_norm[:, v % 2, :, :].rearrange("p a c -> p (a c)"),
                                   v_back[:, :, :].rearrange("p j c -> p (j c)"), ALU.mult).then_inc(back_done, 1)
                pool.wait_ge(back_done, base + (v + 1))
                pool.wait_ge(xb_done, base + (v + 1))
                if not known_below(base, 4 - v):
                    pool.wait_ge(stored[m // 2], 4 * g)
                pool.tensor_tensor(y_ring[:, m, :], xb_ring[:, m, :], o_back[:, v % 2, :],
                                   ALU.add).then_inc(y_done, 1)

            pool.memset(ident[:, :], 0.0).then_inc(const_done, 1)
            pool.memset(mean_of[:, :], 1.0 / (2 * P)).then_inc(const_done, 1)
            pool.memset(var_of[:, :], 1.0 / NORM_COUNT).then_inc(const_done, 1)
            pool.wait_ge(const_done, 3)
            pool.affine_select(out=ident[:, :], in_=ident[:, :], compare_op=ALU.not_equal, fill=1.0, base=0,
                               pattern=[[-1, P]], channel_multiplier=1).then_inc(const_done, 1)
            for m in range(4):
                pool.memset(v_hi[:, m, :, :, HC:HC + 1], 1.0).then_inc(const_done, 1)
                pool.memset(v_lo[:, m, :, :, HC:HC + 1], 0.0).then_inc(const_done, 1)
            pool.wait_ge(setup_dve, 15)
            def order(run, next_image):
                run(-2, v_low)
                run(0, add_bias)
                run(-3, finish)

            schedule(pool, order)


_INS = ["x", "L0_conv_W_qkv", "L0_conv_b_qkv"]


def kernel(**inputs):
    import numpy as _np
    import concourse.bacc as _bacc
    from concourse import mybir as _mybir
    from concourse.bass_utils import run_bass_kernel_spmd as _run

    nc = _bacc.Bacc("TRN2", target_bir_lowering=False, num_devices=1)
    arrays, args = {}, []
    for name in _INS:
        a = _np.ascontiguousarray(inputs[name])
        arrays[f"in_{name}_dram"] = a
        args.append(nc.dram_tensor(f"in_{name}_dram", a.shape, _mybir.dt.from_np(a.dtype), kind="ExternalInput").ap())
    shape = inputs["x"].shape
    args.append(nc.dram_tensor("out_0_dram", shape, _mybir.dt.float32, kind="ExternalOutput").ap())
    groupnorm_attention(nc, *args)
    r = _run(nc, [arrays], core_ids=[0])
    return r.results[0]["out_0_dram"]
```
